# Optimizing a Trainium2 kernel written in Bass

```python
import numpy as np
import jax
import jax.numpy as jnp

def _softmax(x, axis=-1):
    return jax.nn.softmax(x, axis=axis)

def _gelu(x):
    return jax.nn.gelu(x, approximate=True)

def _silu(x):
    return jax.nn.silu(x)

def _sigmoid(x):
    return jax.nn.sigmoid(x)

def _layernorm(x, axis=-1, eps=1e-05):
    m = jnp.mean(x, axis=axis, keepdims=True)
    v = jnp.var(x, axis=axis, keepdims=True)
    return (x - m) / jnp.sqrt(v + eps)

def _scatter_add(tgt, idx, src, axis=0):
    return tgt.at[idx].add(src)

def _segment_sum(src, seg, n):
    return jax.ops.segment_sum(src, seg, n)
kernel_name = 'mk_cond_resid_d2_seqx_r8_72fc25'

def setup_inputs(seed: int=0):
    np.random.seed(seed)
    _w = jnp.asarray

    def _rec_inputs():
        import jax
        import jax.numpy as jnp
        _rk = jax.random.key(seed)
        x = -0.000125 + 0.9999 * jax.random.normal(jax.random.fold_in(_rk, 1), (64, 32, 512), jnp.float32)
        _lenS = 32 - jax.random.randint(jax.random.fold_in(_rk, 7), (64,), 0, max(1, 32 // 4) + 1, jnp.int32)
        _lenS2 = 32 - jax.random.randint(jax.random.fold_in(_rk, 8), (64,), 0, max(1, 32 // 4) + 1, jnp.int32)
        condB_codebook = -0.0625 + 0.715345 * jax.random.normal(jax.random.fold_in(_rk, 11), (64,), jnp.float32)
        itok_B_0_15 = jax.random.randint(jax.random.fold_in(_rk, 12), (64,), 0, 16, jnp.int32)
        return (x, condB_codebook, itok_B_0_15)
    x, condB_codebook, itok_B_0_15 = _rec_inputs()

    def _L0_cond_setup():
        import jax, jax.numpy as jnp
        import numpy as np
        GROUP = 128
        LORA_ALPHA = 32.0
        LORA_RANK = 64
        key = jax.random.key(seed)
        k1, k2, k3, k4 = jax.random.split(key, 4)
        O, I = (512, 512)
        x = jax.random.normal(k1, (4, 256, I), dtype=jnp.float32)
        weight = jax.random.normal(k2, (O, I), dtype=jnp.float32) * 0.02
        wg = weight.reshape(O, I // GROUP, GROUP)
        scale_log = jnp.log(jnp.clip(jnp.max(jnp.abs(wg), axis=2, keepdims=True), 1e-05))
        codebook = jnp.array([-1.0, -0.25, 0.0, 1.0], dtype=jnp.float32)
        lora_A = jax.random.normal(k3, (LORA_RANK, I), dtype=jnp.float32) * 0.02
        lora_B = jax.random.normal(k4, (O, LORA_RANK), dtype=jnp.float32) * 0.02
        return {'x': x, 'weight': weight, 'scale_log': scale_log, 'codebook': codebook, 'lora_A': lora_A, 'lora_B': lora_B}
    _L0_cond_all = _L0_cond_setup()
    _L0_cond_in = {k: v for k, v in _L0_cond_all.items() if k in ('weight', 'scale_log', 'lora_A', 'lora_B')}
    del _L0_cond_all

    def _L1_cond_setup():
        import jax, jax.numpy as jnp
        import numpy as np
        MAX_LORAS = 16
        IN, OUT = (512, 512)
        B, S = (8, 256)
        key = jax.random.key(seed)
        k1, k2, k3 = jax.random.split(key, 3)
        x = jax.random.normal(k1, (B, S, IN), dtype=jnp.float32)
        adapter_ids = jax.random.randint(k2, (B,), 0, MAX_LORAS)
        weight = jax.random.normal(k3, (MAX_LORAS, OUT, IN), dtype=jnp.float32) * 0.02
        return {'x': x, 'adapter_ids': adapter_ids, 'weight': weight}
    _L1_cond_all = _L1_cond_setup()
    _L1_cond_in = {k: v for k, v in _L1_cond_all.items() if k in ('weight',)}
    del _L1_cond_all
    return {'x': x, 'condB_codebook': condB_codebook, 'itok_B_0_15': itok_B_0_15, 'L0_cond_weight': _L0_cond_in['weight'], 'L0_cond_scale_log': _L0_cond_in['scale_log'], 'L0_cond_lora_A': _L0_cond_in['lora_A'], 'L0_cond_lora_B': _L0_cond_in['lora_B'], 'L1_cond_weight': _L1_cond_in['weight']}

def reference(x, condB_codebook, itok_B_0_15, L0_cond_weight, L0_cond_scale_log, L0_cond_lora_A, L0_cond_lora_B, L1_cond_weight):
    import jax
    import jax.numpy as jnp

    def _L0_cond_ref(x, weight, scale_log, codebook, lora_A, lora_B):
        import jax, jax.numpy as jnp
        import numpy as np
        GROUP = 128
        LORA_ALPHA = 32.0
        LORA_RANK = 64
        O, I = weight.shape
        lora_delta = lora_B @ lora_A * (LORA_ALPHA / LORA_RANK)
        cb = codebook / jnp.clip(jnp.max(jnp.abs(codebook)), 1e-08)
        scale = jnp.exp(scale_log)
        wg = (weight + lora_delta).reshape(O, I // GROUP, GROUP)
        normalized = wg / scale
        thresholds = (cb[:-1] + cb[1:]) * 0.5
        idx = jnp.searchsorted(thresholds, normalized, side='left')
        quantized = cb[idx]
        w = jax.lax.stop_gradient(quantized - normalized) + normalized
        w_q = (w * scale).reshape(O, I)
        w_eff = w_q + lora_delta
        return x @ w_eff.T

    def _L1_cond_ref(x, adapter_ids, weight):
        import jax, jax.numpy as jnp
        import numpy as np
        MAX_LORAS = 16
        IN, OUT = (512, 512)
        B, S = (8, 256)
        w = weight[adapter_ids]
        return jnp.einsum('bsi,boi->bso', x, w)
    x = x + _L0_cond_ref(x, L0_cond_weight, L0_cond_scale_log, condB_codebook, L0_cond_lora_A, L0_cond_lora_B)
    x = x + _L1_cond_ref(x, itok_B_0_15, L1_cond_weight)
    return x

_drawn_inputs = setup_inputs


def setup_inputs(seed=0):
    import zlib

    import numpy as np

    out = dict(_drawn_inputs(seed))
    spreads = {}
    factors = {}
    for name, (base, spread) in spreads.items():
        noise = np.random.default_rng([zlib.crc32(name.encode()), seed]).standard_normal(out[name].shape)
        drawn = base * np.exp(spread * noise) if base else spread * noise
        out[name] = jnp.asarray(drawn.astype(out[name].dtype))
    for name, factor in factors.items():
        out[name] = (out[name] * factor).astype(out[name].dtype)
    return out
```

```python
from contextlib import ExitStack

import concourse.bass as bass
from concourse import mybir

F32 = mybir.dt.float32
F32R = mybir.dt.float32r
I32 = mybir.dt.int32
U8 = mybir.dt.uint8
ALU = mybir.AluOpType
ACT = mybir.ActivationFunctionType
AX = mybir.AxisListType.X

P = 128
B = 64
S = 32
D = 512
K = D // P
NA = 16
RANK = 64
NC = 64
LEVELS = 6
TB = P // S
MAX_TILES = NA + (B - NA) // TB
CHUNKS = 4
CB = B // CHUNKS
BLK = K * S
ROW = K * D
RAW = 3
RING = 6
FIRST = 2
ON_DVE = (2, 3, 4)
ON_POOL = tuple(a for a in range(NA) if a not in ON_DVE)
KEEP = 8
BIG = 3.0e38


def adapter_mlp(nc, x, codebook, ids, w0, scale_log, lora_a, lora_bt, w1, out):
    ctx = ExitStack()
    with ctx:
        def sb(name, shape, dt=F32):
            return ctx.enter_context(nc.sbuf_tensor(name, shape, dt))

        def sem(name):
            return ctx.enter_context(nc.semaphore(name))

        x1 = sb("x1", [P, (B + 1) * BLK])
        pairs = sb("pairs", [P, RING * 2 * ROW], F32R)
        assert FIRST + CHUNKS == RING and CB * BLK == ROW
        raw = sb("raw", [P, RAW, ROW])
        inv_scale = raw[:, 1, :].rearrange("p (m n) -> p m n", m=K)
        w0_sb = sb("w0_sb", [P, K, D])
        scale = sb("scale", [P, K, D])
        la = sb("la", [RANK, D])
        lb = sb("lb", [RANK, D])
        norm = w0_sb
        y = sb("y", [P, 2, D])
        quant, weff = y[:, 0, :], y[:, 1, :]
        masks = sb("masks", [P, 2, D], U8)
        w0_hi = sb("w0_hi", [P, 2, D], F32R)
        w0_lo = sb("w0_lo", [P, 2, D], F32R)
        tile_hi = sb("tile_hi", [P, 2, D], F32R)
        tile_lo = sb("tile_lo", [P, 2, D], F32R)
        ident = sb("ident", [P, P])
        cbk = sb("cbk", [P, NC])
        cb = sb("cb", [P, NC])
        cmax = sb("cmax", [P, 2])
        thr = sb("thr", [P, NC])
        upper = sb("upper", [P, NC])
        lower = sb("lower", [P, NC])
        key = sb("key", [P, NC])
        key2 = sb("key2", [P, NC])
        scratch = sb("scratch", [P, NA * B])
        hit = scratch[:, 0:KEEP * NC].rearrange("p (r n) -> p r n", r=KEEP)
        one_hit = sb("one_hit", [P, 2, NC])
        steps = sb("steps", [P, NC])
        step_cb = sb("step_cb", [P, NC])
        more_mask = sb("more_mask", [P, D], U8)
        found = sb("found", [P, KEEP])
        found_cb = sb("found_cb", [P, KEEP])
        one_step = sb("one_step", [P, 2])
        odd = sb("odd", [1, 16])
        is_adapter = sb("is_adapter", [B, NA])
        n_steps = sb("n_steps", [P, 1])
        n_steps_i = sb("n_steps_i", [P, 1], I32)
        id_row_i = sb("id_row_i", [B, B], I32)
        id_col_i = sb("id_col_i", [B, 1], I32)
        id_row = sb("id_row", [B, B])
        id_col = sb("id_col", [B, 1])
        key_row = sb("key_row", [B, B])
        key_col = sb("key_col", [B, 1])
        smaller = sb("smaller", [B, 2, B])
        pos_less = sb("pos_less", [B, 2])
        rank = sb("rank", [B, 1])
        is_id = scratch[0:B, :].rearrange("p (a b) -> p a b", a=NA)
        count = sb("count", [B, NA])
        filled = scratch[0:B, 0:NA * NA].rearrange("p (a b) -> p a b", a=NA)
        tiles = sb("tiles", [B, NA])
        tile_end = sb("tile_end", [B, 2, NA])
        tile_beg = sb("tile_beg", [B, NA])
        beg_of = sb("beg_of", [B, NA])
        beg_b = sb("beg_b", [B, 1])
        slot = sb("slot", [B, 1])
        at_slot = sb("at_slot", [B, MAX_TILES * TB])
        before = scratch[0:1, 0:MAX_TILES * NA].rearrange("p (t a) -> p t a", a=NA)
        adapter = sb("adapter", [1, MAX_TILES])
        adapter_part = sb("adapter_part", [1, 3, MAX_TILES])
        tile_i = sb("tile_i", [1, MAX_TILES, 2], I32)
        end_i = sb("end_i", [1, NA], I32)
        last_pair_f = sb("last_pair_f", [1, 1])
        last_pair_i = sb("last_pair_i", [1, 2], I32)
        batch_i = sb("batch_i", [1, MAX_TILES * TB], I32)
        i_row = sb("i_row", [P, NC])
        i_col = sb("i_col", [P, 1])
        i_col_b = sb("i_col_b", [P, 1])
        i_slot = sb("i_slot", [B, MAX_TILES * TB])
        i_tile = sb("i_tile", [1, MAX_TILES])
        i_tiles4 = sb("i_tiles4", [B, NA])

        ps0 = ctx.enter_context(nc.psum_tensor("ps0", [P, CHUNKS, D], F32))
        ps_t = ctx.enter_context(nc.psum_tensor("ps_t", [P, 2, D], F32))
        ps_d = ctx.enter_context(nc.psum_tensor("ps_d", [P, 2, D], F32))
        batch_ps = ps_t[0:1, 0, 0:MAX_TILES * TB]
        val_ps = ps_t[:, 1, 0:KEEP]

        ids_in, cb_in, lora_in = (sem(n) for n in ("ids_in", "cb_in", "lora_in"))
        w0_in = [sem(f"w0_in{i}") for i in range(2)]
        slog_in = [sem(f"slog_in{i}") for i in range(2)]
        x_in = [sem(f"x_in{c}") for c in range(CHUNKS)]
        raw_in = [sem(f"raw_in{r}") for r in range(RAW)]
        consts = sem("consts")
        pool_step = sem("pool_step")
        ident_ready = sem("ident_ready")
        dve_step = sem("dve_step")
        slots_ready = sem("slots_ready")
        slots_ps = sem("slots_ps")
        tables_ready = sem("tables_ready")
        batches_ready = sem("batches_ready")
        scale_ready = sem("scale_ready")
        delta_ready = sem("delta_ready")
        sum_ready = sem("sum_ready")
        norm_ready = sem("norm_ready")
        steps_ready = sem("steps_ready")
        weff_ready = sem("weff_ready")
        w0_hi_ready = sem("w0_hi_ready")
        w0_ready = sem("w0_ready")
        x_hi_ready = sem("x_hi_ready")
        x_ready = sem("x_ready")
        l0_done = sem("l0_done")
        x1_ready = sem("x1_ready")
        eye_pool = sem("eye_pool")
        eye_dve = sem("eye_dve")
        w_hi_ready = sem("w_hi_ready")
        split_pool = sem("split_pool")
        split_dve = sem("split_dve")
        tile_hi_ready = sem("tile_hi_ready")
        tile_ready = sem("tile_ready")
        tiles_done = sem("tiles_done")
        y_ready = sem("y_ready")
        all_stored = sem("all_stored")
        stored = [sem(f"stored{i}") for i in range(2)]

        def ring_slot(a):
            at = a % RING * 2 * ROW
            return pairs[:, at:at + ROW], pairs[:, at + ROW:at + 2 * ROW]

        def wait_for(eng, a, on_pool, on_dve):
            if a in ON_POOL:
                eng.wait_ge(on_pool, ON_POOL.index(a) + 1)
            else:
                eng.wait_ge(on_dve, ON_DVE.index(a) + 1)

        def add_eye(engine, a):
            r = raw[:, a % RAW, :]
            d = bass.AP(r.tensor, r.offset, [list(r.ap[0]), [D + P, K], [1, P]])
            eye = ident[:, :].rearrange("p (o n) -> p o n", o=1).broadcast_to([P, K, P])
            return engine.tensor_tensor(d, d, eye, ALU.add)

        def w_low(engine, a):
            hi, lo = ring_slot(a)
            return engine.tensor_tensor(lo, raw[:, a % RAW, :], hi.bitcast(F32), ALU.subtract)

        def load_values(eng, at, least, most):
            return nc.values_load_multi_w_load_instructions(at, engines=[eng.engine], min_val=least, max_val=most)[1]

        def load_batches(eng, t):
            return load_values(eng, batch_i[0:1, bass.ds(t * TB, TB)], 0, B)

        block = ctx.enter_context(nc.Block())

        @block.sync
        def _(sp):
            w0_rows, sc_rows = (z[:, :, :].rearrange("p m n -> p (m n)") for z in (w0_sb, scale))
            sp.dma_start(w0_rows[:, 0:D], w0[:, 0:D]).then_inc(w0_in[0], 16)
            sp.dma_start(w0_rows[:, D:], w0[:, D:]).then_inc(w0_in[1], 16)
            sp.dma_start(sc_rows[:, D:], scale_log[:, D:].broadcast_to([P, ROW - D])).then_inc(slog_in[1], 16)
            for c in range(CHUNKS):
                sp.dma_start(x1[:, c * ROW:(c + 1) * ROW].rearrange("p (q n) -> p q n", n=BLK),
                             x[c * CB:(c + 1) * CB].rearrange("q p n -> p q n")).then_inc(x_in[c], 16)
                if c == 1:
                    sp.dma_start(id_row_i[:, :], ids.rearrange("(a n) -> a n", a=1).broadcast_to([B, B])).then_inc(ids_in, 16)
                    sp.dma_start(id_col_i[:, :], ids.rearrange("(n a) -> n a", a=1)).then_inc(ids_in, 16)
            sp.wait_ge(batches_ready, 1)
            pairs_n = sp.value_load(last_pair_i[0:1, 1:2], min_val=B // TB // 2, max_val=MAX_TILES // 2)
            with sp.Fori(0, pairs_n) as i:
                for h in range(2):
                    to = load_batches(sp, 2 * i + h)
                    sp.wait_ge(y_ready, 2 * i + (h + 1))
                    for j, b in enumerate(to):
                        sp.dma_start(out[bass.ds(b % B, 1)].rearrange("b s n -> (b s) n"), y[S * j:S * j + S, h, :],
                                     cond=b < B).then_inc(stored[h], 16)
            for h in range(2):
                sp.wait_ge(stored[h], pairs_n * (16 * TB))
            sp.sem_inc(all_stored, 1)

        @block.gpsimd
        def _(pool):
            g = nc.gpsimd
            made = [0]

            def link(ins):
                made[0] += 1
                ins.then_inc(pool_step, 1)
                pool.wait_ge(pool_step, made[0])

            def iota(t, pattern, cm=0, base=0):
                g.iota(t, pattern=pattern, base=base, channel_multiplier=cm,
                       allow_small_or_imprecise_dtypes=True).then_inc(consts, 1)

            link(g.memset(ident[:, :], 0.0))
            g.affine_select(out=ident[:, :], in_=ident[:, :], compare_op=ALU.not_equal, fill=1.0, base=0,
                            pattern=[[-1, P]], channel_multiplier=1).then_inc(ident_ready, 1)
            g.memset(x1[:, B * BLK:], 0.0).then_inc(consts, 1)
            iota(i_row[:, :], [[1, NC]])
            iota(i_col[:, :], [[0, 1]], cm=1)
            iota(i_col_b[:, :], [[0, 1]], cm=1, base=-B)
            iota(i_slot[:, :], [[1, MAX_TILES * TB]])
            iota(i_tile[:, :], [[1, MAX_TILES]])
            iota(i_tiles4[:, :], [[TB, NA]])
            pool.wait_ge(consts, 7)
            pool.wait_ge(ident_ready, 1)

            def x_low(c):
                hi, lo = ring_slot(FIRST + c)
                pool.wait_ge(x_hi_ready, c + 1)
                g.tensor_tensor(lo, x1[:, c * ROW:(c + 1) * ROW], hi.bitcast(F32), ALU.subtract).then_inc(x_ready, 1)

            def normalise(m):
                pool.wait_ge(sum_ready, m + 1)
                pool.wait_ge(scale_ready, m + 1)
                g.tensor_tensor(norm[:, m, :], norm[:, m, :], inv_scale[:, m, :], ALU.mult).then_inc(norm_ready, 1)

            def compare(to, a, b, op):
                link(g.tensor_tensor(to, a, b, ALU.subtract))
                link(g.tensor_scalar(to, to, 0.0, None, op))

            def total(to, of, n):
                while n > 2:
                    n //= 2
                    link(g.tensor_tensor(of[:, :, 0:n], of[:, :, 0:n], of[:, :, n:2 * n], ALU.add))
                link(g.tensor_tensor(to.rearrange("p (r o) -> p r o", o=1), of[:, :, 0:1], of[:, :, 1:2], ALU.add))

            def tables():
                pool.wait_ge(ids_in, 32)
                g.tensor_copy(id_row[:, :], id_row_i[:, :])
                link(g.tensor_copy(id_col[:, :], id_col_i[:, :]))
                g.tensor_scalar(key_row[:, :], id_row[:, :], float(B), None, ALU.mult)
                link(g.tensor_scalar(key_col[:, :], id_col[:, :], float(B), None, ALU.mult))
                g.tensor_tensor(key_row[:, :], key_row[:, :], i_row[0:B, :], ALU.add)
                link(g.tensor_tensor(key_col[:, :], key_col[:, :], i_col[0:B, :], ALU.add))
                g.tensor_scalar(smaller[:, 0, :], key_row[:, :], key_col[:, 0:1], None, ALU.is_lt)
                g.tensor_scalar(smaller[:, 1, :], id_row[:, :], id_col[:, 0:1], None, ALU.is_lt)
                compare(is_id[:, :, :],
                        id_row[:, :].rearrange("p (o n) -> p o n", o=1).broadcast_to([B, NA, B]),
                        i_row[0:B, 0:NA].rearrange("p (n o) -> p n o", o=1).broadcast_to([B, NA, B]),
                        ALU.is_equal)
                total(pos_less[:, :], smaller[:, :, :], B)
                total(count[:, :], is_id[:, :, :], B)
                g.tensor_tensor(rank[:, :], pos_less[:, 0:1], pos_less[:, 1:2], ALU.subtract)
                compare(filled[:, :, :],
                        count[:, :].rearrange("p (n o) -> p n o", o=1).broadcast_to([B, NA, NA]),
                        i_tiles4[:, :].rearrange("p (o n) -> p o n", o=1).broadcast_to([B, NA, NA]),
                        ALU.is_gt)
                total(tiles[:, :], filled[:, :, :], NA)
                assert NA == 16
                src = tiles[:, :]
                for n, d in enumerate((1, 2, 4, 8)):
                    dst = tile_end[:, n % 2, :]
                    g.tensor_copy(dst[:, 0:d], src[:, 0:d])
                    link(g.tensor_tensor(dst[:, d:], src[:, d:], src[:, 0:NA - d], ALU.add))
                    src = dst
                ends = src
                g.tensor_scalar(end_i[:, :], ends[0:1, :], 1.0, None, ALU.add)
                g.tensor_scalar(is_adapter[:, :], i_row[0:B, 0:NA], id_col[:, 0:1], None, ALU.is_equal)
                link(g.tensor_tensor(tile_beg[:, :], ends, tiles[:, :], ALU.subtract))
                link(g.tensor_tensor(beg_of[:, :], is_adapter[:, :], tile_beg[:, :], ALU.mult))
                total(beg_b[:, :], beg_of[:, :].rearrange("p (o n) -> p o n", o=1), NA)
                link(g.tensor_scalar(beg_b[:, :], beg_b[:, :], float(TB), None, ALU.mult))
                link(g.tensor_tensor(slot[:, :], beg_b[:, :], rank[:, :], ALU.add))
                g.tensor_scalar(at_slot[:, :], i_slot[:, :], slot[:, 0:1], None, ALU.is_equal).then_inc(slots_ready, 1)
                compare(before, ends[0:1, :].rearrange("p (o n) -> p o n", o=1).broadcast_to([1, MAX_TILES, NA]),
                        i_tile[:, :].rearrange("p (t o) -> p t o", o=1).broadcast_to([1, MAX_TILES, NA]),
                        ALU.is_le)
                total(adapter[:, :], before, NA)
                link(g.tensor_scalar(adapter[:, :], adapter[:, :], float(NA - 1), None, ALU.min))
                own = ON_DVE[0]
                part = adapter_part
                g.tensor_scalar(part[:, 0, :], adapter[:, :], 1.0, float(own), ALU.add, ALU.min)
                g.tensor_scalar(part[:, 1, :], adapter[:, :], -float(ON_DVE[-1]), 0.0, ALU.add, ALU.max)
                assert 2 * RING < NA <= 3 * RING
                link(g.tensor_scalar(part[:, 2, :], adapter[:, :], float(RING), -float(RING), ALU.is_ge, ALU.mult))
                g.tensor_tensor(part[:, 0, :], part[:, 0, :], part[:, 1, :], ALU.add)
                link(g.tensor_tensor(part[:, 2, :], part[:, 2, :], adapter[:, :], ALU.add))
                link(g.tensor_scalar(adapter[:, :], adapter[:, :], float(2 * RING), -float(RING), ALU.is_ge, ALU.mult))
                link(g.tensor_tensor(part[:, 2, :], part[:, 2, :], adapter[:, :], ALU.add))
                g.tensor_copy(tile_i[:, :, 0], part[:, 0, :])
                g.tensor_scalar(tile_i[:, :, 1], part[:, 2, :], float(2 * ROW), None, ALU.mult)
                ODD = 16
                link(g.tensor_scalar(odd[:, :], i_tile[:, 0:ODD], 2.0, 1.0, ALU.mult, ALU.add))
                compare(odd[:, :], odd[:, :], ends[0:1, NA - 1:NA].broadcast_to([1, ODD]), ALU.is_le)
                total(last_pair_f[:, :], odd[:, :].rearrange("p (o n) -> p o n", o=1), ODD)
                g.tensor_copy(last_pair_i[:, 1:2], last_pair_f[:, :])
                g.tensor_scalar(last_pair_i[:, 0:1], last_pair_f[:, :], -1.0, None, ALU.add).then_inc(tables_ready, 1)

            def eye(a):
                pool.wait_ge(raw_in[a % RAW], 16 * (a // RAW + 1))
                add_eye(g, a).then_inc(eye_pool, 1)

            def split(a):
                pool.wait_ge(w_hi_ready, a + 1)
                w_low(g, a).then_inc(split_pool, 1)

            x_low(0)
            x_low(1)
            normalise(1)
            x_low(2)
            x_low(3)
            tables()
            normalise(2)
            eye(0)
            normalise(3)
            eye(1)
            split(0)
            split(1)
            rest = [a for a in ON_POOL if a > 1]
            eye(rest[0])
            for a, following in zip(rest, rest[1:]):
                eye(following)
                split(a)
            split(rest[-1])

        @block.scalar
        def _(act):
            act.dma_start(cbk[:, :], codebook.rearrange("(a n) -> a n", a=1).broadcast_to([P, NC])).then_inc(cb_in, 16)
            act.dma_start(scale[:, 0, :], scale_log[:, 0:D].broadcast_to([P, D])).then_inc(slog_in[0], 16)
            act.dma_start(la[:, :], lora_a).then_inc(lora_in, 16)
            act.dma_start(lb[:, :], lora_bt).then_inc(lora_in, 16)

            def scales(m):
                act.wait_ge(slog_in[min(m, 1)], 16)
                nc.scalar.activation(inv_scale[:, m, :], scale[:, m, :], ACT.Exp, scale=-1.0)
                nc.scalar.activation(scale[:, m, :], scale[:, m, :], ACT.Exp).then_inc(scale_ready, 1)

            def load_w(a):
                if a == 1:
                    act.wait_ge(norm_ready, K - 1)
                if a >= RAW:
                    wait_for(act, a - RAW, split_pool, split_dve)
                act.dma_start(raw[:, a % RAW, :], w1[a]).then_inc(raw_in[a % RAW], 16)

            def x_high(c):
                act.wait_ge(x_in[c], 16)
                nc.scalar.activation(ring_slot(FIRST + c)[0], x1[:, c * ROW:(c + 1) * ROW],
                                     ACT.Copy).then_inc(x_hi_ready, 1)

            def w0_high(m):
                act.wait_ge(weff_ready, m + 1)
                if m >= 2:
                    act.wait_ge(l0_done, CHUNKS * (m - 1))
                nc.scalar.activation(w0_hi[:, m % 2, :], weff, ACT.Copy).then_inc(w0_hi_ready, 1)

            def x1_out(m, c):
                to = x1[:, bass.ds(c * ROW, ROW)].rearrange("p (q k s) -> p q k s", k=K, s=S)[:, :, m, :]
                nc.scalar.activation(to, ps0[:, bass.ds(c, 1), :].rearrange("p c (q s) -> p (c q) s", s=S),
                                     ACT.Copy).then_inc(x1_ready, 1)

            def x1_block(m):
                with act.Fori(0, CHUNKS) as c:
                    act.wait_ge(l0_done, c + (CHUNKS * m + 1))
                    x1_out(m, c)

            def w_high(a):
                wait_for(act, a, eye_pool, eye_dve)
                if a >= RING:
                    end = act.value_load(end_i[0:1, a - RING:a - RING + 1], min_val=1, max_val=MAX_TILES + 1)
                    act.wait_ge(tiles_done, end)
                nc.scalar.activation(ring_slot(a)[0], raw[:, a % RAW, :], ACT.Copy).then_inc(w_hi_ready, 1)

            scales(0)
            x_high(0)
            scales(1)
            x_high(1)
            load_w(0)
            load_w(2)
            w0_high(0)
            x_high(2)
            x_high(3)
            scales(2)
            scales(3)
            w0_high(1)
            x1_block(0)
            w_high(0)
            w0_high(2)
            load_w(1)
            x1_block(1)
            w_high(1)
            w0_high(3)
            load_w(3)
            load_w(4)
            x1_block(2)
            for c in range(CHUNKS):
                act.wait_ge(l0_done, CHUNKS * (K - 1) + c + 1)
                x1_out(K - 1, c)
                if c < CHUNKS - 1:
                    w_high(FIRST + c)
                    load_w(FIRST + c + RAW)
            act.wait_ge(tables_ready, 1)
            for a in range(RING - 1, NA):
                w_high(a)
                if a + RAW < NA:
                    load_w(a + RAW)

        @block.vector
        def _(dve):
            made = [0]

            def link(ins):
                made[0] += 1
                ins.then_inc(dve_step, 1)
                dve.wait_ge(dve_step, made[0])

            v = nc.vector
            v.memset(upper[:, :], BIG)
            v.memset(lower[:, :], -BIG)
            dve.wait_ge(cb_in, 16)
            link(v.tensor_reduce(cmax[:, 0:1], cbk[:, :], AX, ALU.max, apply_absolute_value=True))
            link(v.tensor_scalar(cmax[:, 1:2], cmax[:, 0:1], 1e-8, None, ALU.max))
            link(v.reciprocal(cmax[:, 0:1], cmax[:, 1:2]))
            link(v.tensor_scalar(cb[:, :], cbk[:, :], cmax[:, 0:1], None, ALU.mult))
            link(v.tensor_tensor(thr[:, 0:NC - 1], cb[:, 0:NC - 1], cb[:, 1:NC], ALU.add))
            link(v.tensor_scalar(thr[:, 0:NC - 1], thr[:, 0:NC - 1], 0.5, None, ALU.mult))
            for level in range(LEVELS):
                nodes, half = 1 << level, NC >> (level + 1)
                up = upper[:, :].rearrange("p (n s h) -> p n s h", s=2, h=half)[:, :, 0, :]
                lo = lower[:, :].rearrange("p (n s h) -> p n s h", s=2, h=half)[:, :, 1, :]
                mid = thr[:, half - 1:NC - 1:2 * half]
                mid = mid.rearrange("p (n o) -> p n o", o=1).broadcast_to([P, nodes, half])
                v.tensor_tensor(up, up, mid, ALU.min)
                link(v.tensor_tensor(lo, lo, mid, ALU.max))
            link(v.tensor_tensor(key2[:, :], lower[:, :], upper[:, :], ALU.is_lt))
            link(v.memset(key2[:, NC - 1:NC], 0.0))
            link(v.tensor_tensor(key[:, :], key2[:, :], upper[:, :], ALU.mult))
            v.tensor_reduce(n_steps[:, :], key2[:, :], AX, ALU.add)
            link(v.tensor_scalar(key2[:, :], key2[:, :], BIG, BIG, ALU.mult, ALU.subtract))
            link(v.tensor_tensor(key[:, :], key[:, :], key2[:, :], ALU.add))
            v.tensor_copy(n_steps_i[:, :], n_steps[:, :])
            link(v.max(steps[:, 0:KEEP], key[:, :]))

            def all_hits(at):
                settle(v.tensor_tensor(hit[:, :, :], key[:, :].rearrange("p (o n) -> p o n", o=1).broadcast_to([P, KEEP, NC]),
                                       at.rearrange("p (r o) -> p r o", o=1).broadcast_to([P, KEEP, NC]), ALU.is_equal))
                settle(v.tensor_tensor(hit[:, :, :], hit[:, :, :],
                                       cb[:, :].rearrange("p (o n) -> p o n", o=1).broadcast_to([P, KEEP, NC]), ALU.mult))

            def settle(ins):
                dve.drain()

            steps_n = dve.value_load(n_steps_i[0:1, 0:1], min_val=0, max_val=NC)
            with dve.If(steps_n > KEEP):
                v.tensor_copy(found[:, :], steps[:, 0:KEEP])
                settle(v.tensor_copy(key2[:, :], key[:, :]))
                with dve.Fori(1, NC // KEEP) as r:
                    settle(v.match_replace(key2[:, :], found[:, :], key2[:, :], -BIG))
                    settle(v.max(found[:, :], key2[:, :]))
                    all_hits(found[:, :])
                    settle(v.tensor_reduce(found_cb[:, :], hit[:, :, :], AX, ALU.add))
                    v.tensor_copy(steps[:, bass.ds(r * KEEP, KEEP)], found[:, :])
                    settle(v.tensor_copy(step_cb[:, bass.ds(r * KEEP, KEEP)], found_cb[:, :]))

            def add_delta(m):
                dve.wait_ge(delta_ready, m + 1)
                if m <= 1:
                    dve.wait_ge(w0_in[m], 16)
                v.scalar_tensor_tensor(norm[:, m, :], ps_d[:, m % 2, :], 0.5, w0_sb[:, m, :], ALU.mult,
                                       ALU.add).then_inc(sum_ready, 1)

            def quantise(m):
                q, n = quant, norm[:, m, :]
                if m >= 1:
                    dve.wait_ge(norm_ready, m)
                link(v.tensor_copy(q, cb[:, NC - 1:NC].broadcast_to([P, D])))
                for r in range(KEEP):
                    if m == 0:
                        v.scalar_tensor_tensor(one_hit[:, r % 2, :], key[:, :], steps[:, r:r + 1], cb[:, :],
                                               ALU.is_equal, ALU.mult, accum_out=step_cb[:, r:r + 1])
                    link(v.tensor_scalar(masks[:, r % 2, :], n, steps[:, r:r + 1], None, ALU.is_le))
                    if m == 0:
                        link(v.tensor_copy(val_ps[:, r:r + 1], step_cb[:, r:r + 1]))
                    link(v.copy_predicated(q, masks[:, r % 2, :], val_ps[:, r:r + 1].broadcast_to([P, D])))
                with dve.If(steps_n > KEEP):
                    with dve.Fori(KEEP, NC) as r:
                        v.tensor_copy(one_step[:, 0:1], steps[:, bass.ds(r, 1)])
                        settle(v.tensor_copy(one_step[:, 1:2], step_cb[:, bass.ds(r, 1)]))
                        settle(v.tensor_scalar(more_mask[:, :], n, one_step[:, 0:1], None, ALU.is_le))
                        settle(v.copy_predicated(q, more_mask[:, :], one_step[:, 1:2].broadcast_to([P, D])))
                link(v.tensor_tensor(q, q, n, ALU.subtract))
                link(v.tensor_tensor(q, q, n, ALU.add))
                link(v.tensor_tensor(q, q, scale[:, m, :], ALU.mult))
                link(v.scalar_tensor_tensor(weff, ps_d[:, m % 2, :], 0.5, q, ALU.mult, ALU.add))
                dve.wait_ge(ident_ready, 1)
                v.tensor_tensor(weff[:, m * P:(m + 1) * P], weff[:, m * P:(m + 1) * P], ident[:, :],
                                ALU.add).then_inc(weff_ready, 1)

            def w0_low(m):
                dve.wait_ge(w0_hi_ready, m + 1)
                if m >= 2:
                    dve.wait_ge(l0_done, CHUNKS * (m - 1))
                v.tensor_tensor(w0_lo[:, m % 2, :], weff, w0_hi[:, m % 2, :].bitcast(F32),
                                ALU.subtract).then_inc(w0_ready, 1)

            add_delta(0)
            add_delta(1)
            dve.wait_ge(sum_ready, 1)
            dve.wait_ge(scale_ready, 1)
            link(v.tensor_tensor(norm[:, 0, :], norm[:, 0, :], inv_scale[:, 0, :], ALU.mult))
            for m in range(K):
                quantise(m)
                w0_low(m)
                if m + 2 < K:
                    add_delta(m + 2)

            def eye(a):
                dve.wait_ge(raw_in[a % RAW], 16 * (a // RAW + 1))
                add_eye(v, a).then_inc(eye_dve, 1)

            eye(ON_DVE[0])
            dve.wait_ge(slots_ps, 1)
            v.tensor_scalar(batch_i[:, :], batch_ps, float(B), None, ALU.add).then_inc(batches_ready, 1)
            for a in ON_DVE:
                if a + 1 in ON_DVE:
                    eye(a + 1)
                dve.wait_ge(w_hi_ready, a + 1)
                w_low(v, a).then_inc(split_dve, 1)

            def place(parts, h, j):
                return parts[:, h, :].rearrange("p (k q s) -> p k q s", k=K, s=S)[:, :, j, :]

            def batch_of(b):
                return x1[:, bass.ds(b * BLK, BLK)].rearrange("p (k s) -> p k s", s=S)

            def tile_parts(t, h):
                batches = load_batches(dve, t)
                for j, b in enumerate(batches):
                    v.tensor_copy(place(tile_hi, h, j), batch_of(b)).then_inc(tile_hi_ready, 1)
                dve.wait_ge(tile_hi_ready, TB * t + TB)
                for j, b in enumerate(batches):
                    hi = place(tile_hi, h, j)
                    v.tensor_tensor(place(tile_lo, h, j), batch_of(b), hi.bitcast(F32), ALU.subtract).then_inc(tile_ready, 1)

            def tile_out(done, h, stores):
                dve.wait_ge(tiles_done, done)
                if stores is not None:
                    dve.wait_ge(stored[h], stores)
                v.tensor_copy(y[:, h, :], ps_t[:, h, :]).then_inc(y_ready, 1)

            last_pair = dve.value_load(last_pair_i[0:1, 0:1], min_val=B // TB // 2 - 1, max_val=MAX_TILES // 2 - 1)
            dve.wait_ge(x1_ready, CHUNKS * K)
            for t in (0, 1):
                tile_parts(t, t)
            for t in (2, 3):
                tile_out(t, t % 2, None)
                tile_parts(t, t % 2)
            with dve.Fori(1, last_pair) as i:
                for h in range(2):
                    t = 2 * i + (2 + h)
                    tile_out(t, h, i * (16 * TB))
                    tile_parts(t, h)
            for h in range(2):
                tile_out(2 * last_pair + (2 + h), h, last_pair * (16 * TB))

        @block.tensor
        def _(pe):
            mm = nc.tensor.matmul
            pe.nop().then_inc(tiles_done, 1)

            def delta(m):
                if m == 0:
                    pe.wait_ge(lora_in, 32)
                if m >= 2:
                    pe.wait_ge(weff_ready, m - 1)
                for k in range(K):
                    last = mm(ps_d[:, m % 2, k * P:(k + 1) * P], la[:, k * P:(k + 1) * P], lb[:, m * P:(m + 1) * P],
                              start=True, stop=True)
                last.then_inc(delta_ready, 1)

            def layer0(m):
                pe.wait_ge(w0_ready, m + 1)
                parts = ((w0_hi, 0), (w0_lo, 0), (w0_hi, ROW))
                with pe.Fori(0, CHUNKS) as c:
                    if m == 0:
                        pe.wait_ge(x_ready, c + 1)
                    else:
                        pe.wait_ge(x1_ready, c + (CHUNKS * (m - 1) + 1))
                    for n, (w, low) in enumerate(parts):
                        for k in range(K):
                            cols = pairs[:, bass.ds(c * (2 * ROW) + (FIRST * 2 * ROW + low), ROW)].rearrange("p (q k s) -> p q k s", k=K, s=S)
                            last = mm(ps0[:, bass.ds(c, 1), :].rearrange("p c n -> p (c n)"),
                                      w[:, m % 2, k * P:(k + 1) * P], cols[:, :, k, :],
                                      start=(n == 0 and k == 0), stop=(n == 2 and k == K - 1))
                    last.then_inc(l0_done, 1)

            delta(0)
            delta(1)
            for m in range(K):
                layer0(m)
                if m + 2 < K:
                    delta(m + 2)
                if m == K - 2:
                    pe.wait_ge(slots_ready, 1)
                    mm(batch_ps, i_col_b[0:B, :], at_slot[:, :], start=True, stop=True).then_inc(slots_ps, 1)

            pe.wait_ge(tables_ready, 1)
            pairs_n = pe.value_load(last_pair_i[0:1, 1:2], min_val=B // TB // 2, max_val=MAX_TILES // 2)
            with pe.Fori(0, pairs_n) as i:
                for h in range(2):
                    t = 2 * i + h
                    (need, at) = load_values(pe, tile_i[0:1, bass.ds(t, 1), :].rearrange("p t n -> p (t n)"), 0,
                                             (RING - 1) * 2 * ROW)
                    pe.wait_ge(tile_ready, TB * t + TB)
                    pe.wait_ge(split_pool, need)
                    parts = ((tile_hi, 0), (tile_lo, 0), (tile_hi, ROW))
                    for n, (xs, low) in enumerate(parts):
                        for k in range(K):
                            last = mm(ps_t[:, h, :], xs[:, h, k * P:(k + 1) * P],
                                      pairs[:, bass.ds(at + (low + k * D), D)],
                                      start=(n == 0 and k == 0), stop=(n == 2 and k == K - 1))
                    last.then_inc(tiles_done, 1)


def kernel(x, condB_codebook, itok_B_0_15, L0_cond_weight, L0_cond_scale_log, L0_cond_lora_A, L0_cond_lora_B,
           L1_cond_weight):
    import numpy as np
    import concourse.bacc as bacc
    from concourse.bass_utils import run_bass_kernel_spmd as run

    arrays = {
        "x_t": x.reshape(B, S, K, P).transpose(0, 3, 2, 1).reshape(B, P, BLK),
        "codebook": condB_codebook,
        "ids": itok_B_0_15,
        "w0_t": L0_cond_weight.reshape(K, P, K, P).transpose(3, 0, 2, 1).reshape(P, ROW),
        "scale_log": L0_cond_scale_log.reshape(K, P, K).transpose(0, 2, 1).reshape(1, K * D),
        "lora_a": L0_cond_lora_A,
        "lora_bt": L0_cond_lora_B.T,
        "w1_t": L1_cond_weight.reshape(NA, D, K, P).transpose(0, 3, 2, 1).reshape(NA, P, ROW),
    }
    arrays = {name: np.ascontiguousarray(a) for name, a in arrays.items()}
    nc = bacc.Bacc("TRN2", target_bir_lowering=False, num_devices=1)
    args = [nc.dram_tensor(name, a.shape, mybir.dt.from_np(a.dtype), kind="ExternalInput").ap()
            for name, a in arrays.items()]
    out = nc.dram_tensor("result", (B, S, D), F32, kind="ExternalOutput").ap()
    adapter_mlp(nc, *args, out)
    return run(nc, [arrays], core_ids=[0]).results[0]["result"]
```

```python
from contextlib import ExitStack

import concourse.bass as bass
from concourse import mybir

F32 = mybir.dt.float32
F32R = mybir.dt.float32r
I32 = mybir.dt.int32
U8 = mybir.dt.uint8
ALU = mybir.AluOpType
ACT = mybir.ActivationFunctionType
AX = mybir.AxisListType.X

P = 128
B = 64
S = 32
D = 512
K = D // P
NA = 16
RANK = 64
NC = 64
LEVELS = 6
TB = P // S
MAX_TILES = NA + (B - NA) // TB
CHUNKS = 4
CB = B // CHUNKS
BLK = K * S
ROW = K * D
RAW = 3
RING = 6
FIRST = 2
ON_DVE = (2, 3, 4)
ON_POOL = tuple(a for a in range(NA) if a not in ON_DVE)
TILE_BUFS = 4
YB = 4
TAIL_ON_POOL = (1, 2)
ROUND = float(2 ** 23)
KEEP = 8
BIG = 3.0e38


def adapter_mlp(nc, x, codebook, ids, w0, scales, lora_a, lora_bt, w1, out):
    ctx = ExitStack()
    with ctx:
        def sb(name, shape, dt=F32):
            return ctx.enter_context(nc.sbuf_tensor(name, shape, dt))

        def sem(name):
            return ctx.enter_context(nc.semaphore(name))

        x1 = sb("x1", [P, (B + 1) * BLK])
        pairs = sb("pairs", [P, RING * 2 * ROW], F32R)
        assert FIRST + CHUNKS == RING and CB * BLK == ROW
        raw = sb("raw", [P, RAW, ROW])
        w0_sb = sb("w0_sb", [P, K, D])
        norm = w0_sb
        scale_log = sb("scale_log", [P, K, K])
        scale = sb("scale", [P, K, K])
        inv_scale = sb("inv_scale", [P, K, K])
        delta = sb("delta", [P, K, D])
        y = sb("y", [P, YB, D])
        quant = y
        assert K == YB
        la, lb = y[0:RANK, 1, :], y[0:RANK, 2, :]
        masks = sb("masks", [P, 2, D], U8)
        tile_hi = sb("tile_hi", [P, TILE_BUFS, D], F32R)
        tile_lo = sb("tile_lo", [P, TILE_BUFS, D], F32R)
        w0_hi, w0_lo = tile_hi[:, 2:4, :], tile_lo[:, 2:4, :]
        ident = sb("ident", [P, P])
        cbk = sb("cbk", [P, NC])
        cb = sb("cb", [P, NC])
        cmax = sb("cmax", [P, 2])
        thr = sb("thr", [P, NC])
        upper = sb("upper", [P, NC])
        lower = sb("lower", [P, NC])
        key = sb("key", [P, NC])
        key2 = sb("key2", [P, NC])
        scratch = sb("scratch", [1, MAX_TILES * NA + 3 * MAX_TILES])
        hit = quant[:, K - 1, :].rearrange("p (r n) -> p r n", r=KEEP)
        steps = sb("steps", [P, NC])
        step_cb = sb("step_cb", [P, NC])
        more_mask = masks[:, 0, :]
        found = sb("found", [P, KEEP])
        found_cb = sb("found_cb", [P, KEEP])
        one_step = sb("one_step", [P, 2])
        odd = sb("odd", [1, 16])
        is_adapter = sb("is_adapter", [B, NA])
        n_steps = sb("n_steps", [P, 1])
        n_steps_i = sb("n_steps_i", [P, 1], I32)
        id_col_i = sb("id_col_i", [B, 1], I32)
        id_col = sb("id_col", [B, 1])
        ones = sb("ones", [B, B])
        earlier = sb("earlier", [B, B])
        counts = sb("counts", [B, 2, NA])
        tiles = sb("tiles", [B, NA])
        tile_end = sb("tile_end", [B, 2, NA])
        tile_beg = sb("tile_beg", [B, NA])
        beg_of = sb("beg_of", [B, NA])
        slot = sb("slot", [B, 1])
        before = scratch[0:1, 0:MAX_TILES * NA].rearrange("p (t a) -> p t a", a=NA)
        adapter = sb("adapter", [1, MAX_TILES])
        adapter_part = scratch[0:1, MAX_TILES * NA:].rearrange("p (n t) -> p n t", n=3)
        tile_i = sb("tile_i", [1, MAX_TILES + 2], I32)
        end_i = sb("end_i", [1, NA], I32)
        pairs_f = sb("pairs_f", [1, 1])
        pairs_i = sb("pairs_i", [1, 1], I32)
        batch_f = sb("batch_f", [1, MAX_TILES * TB // 2])
        batch_i = sb("batch_i", [1, MAX_TILES * TB // 2], I32)
        i_row = sb("i_row", [P, NC])
        i_col = sb("i_col", [P, 1])
        i_col_b = sb("i_col_b", [P, 1])
        i_slot = sb("i_slot", [B, MAX_TILES * TB])
        at_slot = i_slot
        i_tile = sb("i_tile", [1, MAX_TILES])

        ps0 = ctx.enter_context(nc.psum_tensor("ps0", [P, CHUNKS, D], F32))
        ps_y = ps0
        assert CHUNKS == YB
        ps_d = ctx.enter_context(nc.psum_tensor("ps_d", [P, 2, D], F32))
        ps_w = ctx.enter_context(nc.psum_tensor("ps_w", [P, D], F32))
        ps_v = ctx.enter_context(nc.psum_tensor("ps_v", [P, D], F32))
        val_ps = ps_v[:, 0:KEEP]
        counts_ps = ps_w[0:B, 0:2 * NA].rearrange("p (n a) -> p n a", n=2)
        batch_ps = ps_d[0:1, 0, 0:MAX_TILES * TB]

        ids_in, cb_in, lora_in = (sem(n) for n in ("ids_in", "cb_in", "lora_in"))
        w0_in = [sem(f"w0_in{i}") for i in range(2)]
        slog_in = sem("slog_in")
        x_in = [sem(f"x_in{c}") for c in range(CHUNKS)]
        raw_in = [sem(f"raw_in{r}") for r in range(RAW)]
        consts = sem("consts")
        pool_step = sem("pool_step")
        ident_ready = sem("ident_ready")
        dve_step = sem("dve_step")
        members_ready = sem("members_ready")
        counts_ps_ready = sem("counts_ps_ready")
        counts_ready = sem("counts_ready")
        slots_ready = sem("slots_ready")
        slots_ps = sem("slots_ps")
        tables_ready = sem("tables_ready")
        batches_ready = sem("batches_ready")
        scale_ready = sem("scale_ready")
        delta_ps = sem("delta_ps")
        delta_ready = sem("delta_ready")
        sum_ready = sem("sum_ready")
        norm_ready = sem("norm_ready")
        quant_ready = sem("quant_ready")
        weff_pool = sem("weff_pool")
        weff_dve = sem("weff_dve")
        turned_ready = sem("turned_ready")
        w0_hi_ready = sem("w0_hi_ready")
        w0_ready = sem("w0_ready")
        x_hi_ready = sem("x_hi_ready")
        x_ready = sem("x_ready")
        l0_done = sem("l0_done")
        x1_ready = sem("x1_ready")
        eye_pool = sem("eye_pool")
        eye_dve = sem("eye_dve")
        w_hi_ready = sem("w_hi_ready")
        split_pool = sem("split_pool")
        split_dve = sem("split_dve")
        tile_hi_ready = sem("tile_hi_ready")
        tile_ready = sem("tile_ready")
        tiles_done = sem("tiles_done")
        y_ready = sem("y_ready")
        y_free = sem("y_free")
        all_stored = sem("all_stored")
        stored = [sem(f"stored{i}") for i in range(2)]

        def ring_slot(a):
            at = a % RING * 2 * ROW
            return pairs[:, at:at + ROW], pairs[:, at + ROW:at + 2 * ROW]

        def wait_for(eng, a, on_pool, on_dve):
            if a in ON_POOL:
                eng.wait_ge(on_pool, ON_POOL.index(a) + 1)
            else:
                eng.wait_ge(on_dve, ON_DVE.index(a) + 1)

        def add_eye(engine, a):
            r = raw[:, a % RAW, :]
            d = bass.AP(r.tensor, r.offset, [list(r.ap[0]), [D + P, K], [1, P]])
            eye = ident[:, :].rearrange("p (o n) -> p o n", o=1).broadcast_to([P, K, P])
            return engine.tensor_tensor(d, d, eye, ALU.add)

        def w_low(engine, a):
            hi, lo = ring_slot(a)
            return engine.tensor_tensor(lo, raw[:, a % RAW, :], hi.bitcast(F32), ALU.subtract)

        def load_values(eng, at, least, most):
            return nc.values_load_multi_w_load_instructions(at, engines=[eng.engine], min_val=least, max_val=most)[1]

        def load_batches(eng, i):
            twos = load_values(eng, batch_i[0:1, bass.ds(i * TB, TB)], 0, (B + 2) * B)
            found = [b for two in twos for b in (two // (B + 1), two % (B + 1))]
            return found[:TB], found[TB:]

        block = ctx.enter_context(nc.Block())

        @block.sync
        def _(sp):
            w0_blocks = w0.rearrange("(m p) n -> p m n", p=P)
            sp.dma_start(la, lora_a).then_inc(lora_in, 16)
            sp.dma_start(lb, lora_bt).then_inc(lora_in, 16)
            sp.dma_start(w0_sb[:, 0, :], w0_blocks[:, 0, :]).then_inc(w0_in[0], 16)
            for c in range(CHUNKS):
                sp.dma_start(x1[:, c * ROW:(c + 1) * ROW].rearrange("p (q n) -> p q n", n=BLK),
                             x[c * CB:(c + 1) * CB].rearrange("q p n -> p q n")).then_inc(x_in[c], 16)
                if c == 0:
                    sp.dma_start(w0_sb[:, 1:, :], w0_blocks[:, 1:, :]).then_inc(w0_in[1], 16)
            sp.sem_inc(y_free, 2)
            for h in range(2):
                sp.sem_inc(stored[h], 1)
            sp.wait_ge(tables_ready, 1)
            sp.wait_ge(batches_ready, 1)
            pairs_n = sp.value_load(pairs_i[0:1, 0:1], min_val=B // TB // 2, max_val=MAX_TILES // 2)
            with sp.Fori(0, pairs_n) as i:
                to = load_batches(sp, i)
                for h in range(2):
                    t = 2 * i + h
                    sp.wait_ge(stored[h], i * (16 * TB) + 1)
                    sp.sem_inc(y_free, 1)
                    sp.wait_ge(y_ready, t + (YB + 1))
                    rows = y[:, bass.ds(t % YB, 1), :].rearrange("p o n -> p (o n)")
                    for j, b in enumerate(to[h]):
                        sp.dma_start(out[bass.ds(b % B, 1)].rearrange("b s n -> (b s) n"), rows[S * j:S * j + S, :],
                                     cond=b < B).then_inc(stored[h], 16)
            for h in range(2):
                sp.wait_ge(stored[h], pairs_n * (16 * TB) + 1)
            sp.sem_inc(all_stored, 1)

        @block.gpsimd
        def _(pool):
            g = nc.gpsimd
            made = [0]

            def link(ins):
                made[0] += 1
                ins.then_inc(pool_step, 1)
                pool.wait_ge(pool_step, made[0])

            def iota(t, pattern, cm=0, base=0):
                g.iota(t, pattern=pattern, base=base, channel_multiplier=cm,
                       allow_small_or_imprecise_dtypes=True).then_inc(consts, 1)

            pool.dma_start(id_col_i[:, :], ids.rearrange("(n a) -> n a", a=1)).then_inc(ids_in, 16)
            link(g.memset(ident[:, :], 0.0))
            g.affine_select(out=ident[:, :], in_=ident[:, :], compare_op=ALU.not_equal, fill=1.0, base=0,
                            pattern=[[-1, P]], channel_multiplier=1).then_inc(ident_ready, 1)
            g.memset(x1[:, B * BLK:], 0.0).then_inc(consts, 1)
            iota(i_row[:, :], [[1, NC]])
            iota(i_col[:, :], [[0, 1]], cm=1)
            iota(i_col_b[:, :], [[0, 1]], cm=1, base=-B)
            iota(i_slot[:, :], [[1, MAX_TILES * TB]])
            iota(i_tile[:, :], [[1, MAX_TILES]])
            g.memset(ones[:, :], 1.0).then_inc(consts, 1)
            pool.wait_ge(consts, 7)
            g.affine_select(out=earlier[:, :], in_=ones[:, :], compare_op=ALU.is_gt, fill=0.0, base=0,
                            pattern=[[1, B]], channel_multiplier=-1).then_inc(consts, 1)

            def x_low(c):
                hi, lo = ring_slot(FIRST + c)
                pool.wait_ge(x_hi_ready, c + 1)
                g.tensor_tensor(lo, x1[:, c * ROW:(c + 1) * ROW], hi.bitcast(F32), ALU.subtract).then_inc(x_ready, 1)

            def tail(m):
                q, n = quant[:, m, :], norm[:, m, :]
                pool.wait_ge(quant_ready, TAIL_ON_POOL.index(m) + 1)
                link(g.tensor_tensor(q, q, n, ALU.subtract))
                link(g.tensor_tensor(q, q, n, ALU.add))
                for k in range(K):
                    cols = q[:, k * P:(k + 1) * P]
                    last = g.tensor_scalar(cols, cols, scale[:, m, k:k + 1], None, ALU.mult)
                link(last)
                g.tensor_tensor(q, q, delta[:, m, :], ALU.add).then_inc(weff_pool, 1)

            def compare(to, a, b, op):
                link(g.tensor_tensor(to, a, b, ALU.subtract))
                link(g.tensor_scalar(to, to, 0.0, None, op))

            def total(to, of, n):
                while n > 2:
                    n //= 2
                    link(g.tensor_tensor(of[:, :, 0:n], of[:, :, 0:n], of[:, :, n:2 * n], ALU.add))
                link(g.tensor_tensor(to.rearrange("p (r o) -> p r o", o=1), of[:, :, 0:1], of[:, :, 1:2], ALU.add))

            def tables():
                pool.wait_ge(ids_in, 16)
                link(g.tensor_copy(id_col[:, :], id_col_i[:, :]))
                pool.wait_ge(consts, 8)
                g.tensor_scalar(is_adapter[:, :], i_row[0:B, 0:NA], id_col[:, 0:1], None,
                                ALU.is_equal).then_inc(members_ready, 1)
                pool.wait_ge(members_ready, 1)
                pool.wait_ge(counts_ready, 1)
                assert TB == 4
                link(g.tensor_scalar(tiles[:, :], counts[:, 0, :], 1.0 / TB, 0.375, ALU.mult, ALU.add))
                link(g.tensor_scalar(tiles[:, :], tiles[:, :], ROUND, None, ALU.add))
                link(g.tensor_scalar(tiles[:, :], tiles[:, :], -ROUND, None, ALU.add))
                assert NA == 16
                src = tiles[:, :]
                for n, d in enumerate((1, 2, 4, 8)):
                    dst = tile_end[:, n % 2, :]
                    g.tensor_copy(dst[:, 0:d], src[:, 0:d])
                    link(g.tensor_tensor(dst[:, d:], src[:, d:], src[:, 0:NA - d], ALU.add))
                    src = dst
                ends = src
                g.tensor_scalar(end_i[:, 0:NA - 1], ends[0:1, 0:NA - 1], 1.0, None, ALU.add)
                link(g.tensor_tensor(tile_beg[:, :], ends, tiles[:, :], ALU.subtract))
                link(g.tensor_scalar(tile_beg[:, :], tile_beg[:, :], float(TB), None, ALU.mult))
                link(g.tensor_tensor(tile_beg[:, :], tile_beg[:, :], counts[:, 1, :], ALU.add))
                link(g.tensor_tensor(beg_of[:, :], is_adapter[:, :], tile_beg[:, :], ALU.mult))
                total(slot[:, :], beg_of[:, :].rearrange("p (o n) -> p o n", o=1), NA)
                g.tensor_scalar(at_slot[:, :], i_slot[:, :], slot[:, 0:1], None, ALU.is_equal).then_inc(slots_ready, 1)
                compare(before, ends[0:1, :].rearrange("p (o n) -> p o n", o=1).broadcast_to([1, MAX_TILES, NA]),
                        i_tile[:, :].rearrange("p (t o) -> p t o", o=1).broadcast_to([1, MAX_TILES, NA]),
                        ALU.is_le)
                total(adapter[:, :], before, NA)
                link(g.tensor_scalar(adapter[:, :], adapter[:, :], float(NA - 1), None, ALU.min))
                own = ON_DVE[0]
                part = adapter_part
                g.tensor_scalar(part[:, 0, :], adapter[:, :], float(own - 1), None, ALU.min)
                g.tensor_scalar(part[:, 1, :], adapter[:, :], -float(ON_DVE[-1]), 0.0, ALU.add, ALU.max)
                assert 2 * RING < NA <= 3 * RING
                link(g.tensor_scalar(part[:, 2, :], adapter[:, :], float(RING), -float(RING), ALU.is_ge, ALU.mult))
                g.tensor_tensor(part[:, 0, :], part[:, 0, :], part[:, 1, :], ALU.add)
                link(g.tensor_tensor(part[:, 2, :], part[:, 2, :], adapter[:, :], ALU.add))
                link(g.tensor_scalar(adapter[:, :], adapter[:, :], float(2 * RING), -float(RING), ALU.is_ge, ALU.mult))
                link(g.tensor_tensor(part[:, 2, :], part[:, 2, :], adapter[:, :], ALU.add))
                link(g.tensor_scalar(part[:, 0, :], part[:, 0, :], float(RING), None, ALU.mult))
                link(g.tensor_tensor(part[:, 0, :], part[:, 0, :], part[:, 2, :], ALU.add))
                g.tensor_copy(tile_i[:, 0:MAX_TILES], part[:, 0, :])
                ODD = 16
                link(g.tensor_scalar(odd[:, :], i_tile[:, 0:ODD], 2.0, 1.0, ALU.mult, ALU.add))
                compare(odd[:, :], odd[:, :], ends[0:1, NA - 1:NA].broadcast_to([1, ODD]), ALU.is_le)
                total(pairs_f[:, :], odd[:, :].rearrange("p (o n) -> p o n", o=1), ODD)
                g.tensor_scalar(end_i[:, NA - 1:NA], pairs_f[:, :], 2.0, 1.0, ALU.mult, ALU.add)
                g.tensor_copy(pairs_i[:, :], pairs_f[:, :]).then_inc(tables_ready, 1)

            def eye(a):
                pool.wait_ge(raw_in[a % RAW], 16 * (a // RAW + 1))
                add_eye(g, a).then_inc(eye_pool, 1)

            def split(a):
                pool.wait_ge(w_hi_ready, a + 1)
                w_low(g, a).then_inc(split_pool, 1)

            tables()
            for c in range(CHUNKS):
                x_low(c)
            pool.wait_ge(delta_ready, K)
            tail(1)
            pool.wait_ge(ident_ready, 1)
            eye(0)
            eye(1)
            tail(2)
            split(0)
            split(1)
            rest = [a for a in ON_POOL if a > 1]
            eye(rest[0])
            for a, following in zip(rest, rest[1:]):
                eye(following)
                split(a)
            split(rest[-1])

        @block.scalar
        def _(act):
            activation = nc.scalar.activation
            act.dma_start(cbk[:, :], codebook.rearrange("(a n) -> a n", a=1).broadcast_to([P, NC])).then_inc(cb_in, 16)
            act.dma_start(scale_log[:, :, :], scales).then_inc(slog_in, 16)

            def load_w(a):
                if a >= RAW:
                    wait_for(act, a - RAW, split_pool, split_dve)
                act.dma_start(raw[:, a % RAW, :], w1[a]).then_inc(raw_in[a % RAW], 16)

            def delta_out(m):
                act.wait_ge(delta_ps, m + 1)
                activation(delta[:, m, :], ps_d[:, m % 2, :], ACT.Copy, scale=0.5).then_inc(delta_ready, 1)

            def normalise(m):
                act.wait_ge(sum_ready, m + 1)
                for k in range(K):
                    cols = norm[:, m, k * P:(k + 1) * P]
                    last = activation(cols, cols, ACT.Copy, scale=inv_scale[:, m, k:k + 1])
                last.then_inc(norm_ready, 1)

            def x_high(c):
                act.wait_ge(x_in[c], 16)
                activation(ring_slot(FIRST + c)[0], x1[:, c * ROW:(c + 1) * ROW], ACT.Copy).then_inc(x_hi_ready, 1)

            def w0_high(m):
                act.wait_ge(turned_ready, m + 1)
                if m >= 2:
                    act.wait_ge(l0_done, CHUNKS * (m - 1))
                activation(w0_hi[:, m % 2, :], ps_w[:, :], ACT.Copy).then_inc(w0_hi_ready, 1)

            def x1_out(m, c):
                to = x1[:, bass.ds(c * ROW, ROW)].rearrange("p (q k s) -> p q k s", k=K, s=S)[:, :, m, :]
                activation(to, ps0[:, bass.ds(c, 1), :].rearrange("p c (q s) -> p (c q) s", s=S),
                           ACT.Copy).then_inc(x1_ready, 1)

            def x1_block(m):
                with act.Fori(0, CHUNKS) as c:
                    act.wait_ge(l0_done, c + (CHUNKS * m + 1))
                    x1_out(m, c)

            def w_high(a):
                wait_for(act, a, eye_pool, eye_dve)
                activation(ring_slot(a)[0], raw[:, a % RAW, :], ACT.Copy).then_inc(w_hi_ready, 1)

            def result(t1):
                act.wait_ge(tiles_done, t1 + TILE_BUFS)
                act.wait_ge(y_free, t1)
                at = bass.ds((t1 + (YB - 1)) % YB, 1)
                activation(y[:, at, :], ps_y[:, at, :], ACT.Copy).then_inc(y_ready, 1)

            act.wait_ge(slog_in, 16)
            activation(inv_scale[:, :, :], scale_log[:, :, :], ACT.Exp, scale=-1.0).then_inc(scale_ready, 1)
            activation(scale[:, :, :], scale_log[:, :, :], ACT.Exp).then_inc(scale_ready, 1)
            act.wait_ge(scale_ready, 2)
            delta_out(0)
            act.wait_ge(counts_ps_ready, 1)
            activation(counts[:, :, :], counts_ps, ACT.Copy).then_inc(counts_ready, 1)
            normalise(0)
            delta_out(1)
            normalise(1)
            delta_out(2)
            delta_out(3)
            for a in range(RAW):
                load_w(a)
            for c in range(CHUNKS):
                x_high(c)
            w0_high(0)
            normalise(2)
            normalise(3)
            x1_block(0)
            w0_high(1)
            x1_block(1)
            w0_high(2)
            w_high(0)
            w_high(1)
            x1_block(2)
            w0_high(3)
            load_w(3)
            load_w(4)
            for c in range(CHUNKS):
                act.wait_ge(l0_done, CHUNKS * (K - 1) + c + 1)
                x1_out(K - 1, c)
                if c == 2:
                    load_w(5)
                if c < CHUNKS - 1:
                    w_high(FIRST + c)
            load_w(RING)
            act.wait_ge(tables_ready, 1)
            act.sem_inc(y_ready, YB)
            begin = 1
            w_high(RING - 1)
            for a in range(NA):
                end = act.value_load(end_i[0:1, a:a + 1], min_val=1, max_val=MAX_TILES + 1)
                with act.If(end > begin):
                    with act.Fori(begin, end) as t1:
                        result(t1)
                begin = end
                if a + RING + 1 < NA:
                    load_w(a + RING + 1)
                if a + RING < NA:
                    w_high(a + RING)

        @block.vector
        def _(dve):
            made = [0]

            def link(ins):
                made[0] += 1
                ins.then_inc(dve_step, 1)
                dve.wait_ge(dve_step, made[0])

            v = nc.vector
            v.memset(upper[:, :], BIG)
            v.memset(lower[:, :], -BIG)
            dve.wait_ge(cb_in, 16)
            link(v.tensor_reduce(cmax[:, 0:1], cbk[:, :], AX, ALU.max, apply_absolute_value=True))
            link(v.tensor_scalar(cmax[:, 1:2], cmax[:, 0:1], 1e-8, None, ALU.max))
            link(v.reciprocal(cmax[:, 0:1], cmax[:, 1:2]))
            link(v.tensor_scalar(cb[:, :], cbk[:, :], cmax[:, 0:1], None, ALU.mult))
            link(v.tensor_tensor(thr[:, 0:NC - 1], cb[:, 0:NC - 1], cb[:, 1:NC], ALU.add))
            link(v.tensor_scalar(thr[:, 0:NC - 1], thr[:, 0:NC - 1], 0.5, None, ALU.mult))
            for level in range(LEVELS):
                nodes, half = 1 << level, NC >> (level + 1)
                up = upper[:, :].rearrange("p (n s h) -> p n s h", s=2, h=half)[:, :, 0, :]
                lo = lower[:, :].rearrange("p (n s h) -> p n s h", s=2, h=half)[:, :, 1, :]
                mid = thr[:, half - 1:NC - 1:2 * half]
                mid = mid.rearrange("p (n o) -> p n o", o=1).broadcast_to([P, nodes, half])
                v.tensor_tensor(up, up, mid, ALU.min)
                link(v.tensor_tensor(lo, lo, mid, ALU.max))
            link(v.tensor_tensor(key2[:, :], lower[:, :], upper[:, :], ALU.is_lt))
            link(v.memset(key2[:, NC - 1:NC], 0.0))
            link(v.tensor_tensor(key[:, :], key2[:, :], upper[:, :], ALU.mult))
            v.tensor_reduce(n_steps[:, :], key2[:, :], AX, ALU.add)
            link(v.tensor_scalar(key2[:, :], key2[:, :], BIG, BIG, ALU.mult, ALU.subtract))
            link(v.tensor_tensor(key[:, :], key[:, :], key2[:, :], ALU.add))
            v.tensor_copy(n_steps_i[:, :], n_steps[:, :])
            link(v.max(steps[:, 0:KEEP], key[:, :]))
            for r in range(KEEP):
                last = v.scalar_tensor_tensor(hit[:, r, :], key[:, :], steps[:, r:r + 1], cb[:, :], ALU.is_equal,
                                              ALU.mult, accum_out=step_cb[:, r:r + 1])
            link(last)
            link(v.tensor_copy(val_ps, step_cb[:, 0:KEEP]))

            def all_hits(at):
                settle(v.tensor_tensor(hit[:, :, :], key[:, :].rearrange("p (o n) -> p o n", o=1).broadcast_to([P, KEEP, NC]),
                                       at.rearrange("p (r o) -> p r o", o=1).broadcast_to([P, KEEP, NC]), ALU.is_equal))
                settle(v.tensor_tensor(hit[:, :, :], hit[:, :, :],
                                       cb[:, :].rearrange("p (o n) -> p o n", o=1).broadcast_to([P, KEEP, NC]), ALU.mult))

            def settle(ins):
                dve.drain()

            steps_n = dve.value_load(n_steps_i[0:1, 0:1], min_val=0, max_val=NC)
            with dve.If(steps_n > KEEP):
                v.tensor_copy(found[:, :], steps[:, 0:KEEP])
                settle(v.tensor_copy(key2[:, :], key[:, :]))
                with dve.Fori(1, NC // KEEP) as r:
                    settle(v.match_replace(key2[:, :], found[:, :], key2[:, :], -BIG))
                    settle(v.max(found[:, :], key2[:, :]))
                    all_hits(found[:, :])
                    settle(v.tensor_reduce(found_cb[:, :], hit[:, :, :], AX, ALU.add))
                    v.tensor_copy(steps[:, bass.ds(r * KEEP, KEEP)], found[:, :])
                    settle(v.tensor_copy(step_cb[:, bass.ds(r * KEEP, KEEP)], found_cb[:, :]))

            def add_delta(m):
                dve.wait_ge(delta_ready, m + 1)
                if m <= 1:
                    dve.wait_ge(w0_in[m], 16)
                v.tensor_tensor(norm[:, m, :], delta[:, m, :], w0_sb[:, m, :], ALU.add).then_inc(sum_ready, 1)

            def first_step(m):
                dve.wait_ge(norm_ready, m + 1)
                v.tensor_copy(quant[:, m, :], cb[:, NC - 1:NC].broadcast_to([P, D]))
                link(v.tensor_scalar(masks[:, 0, :], norm[:, m, :], steps[:, 0:1], None, ALU.is_le))

            def kept_steps(m, begin, end):
                for r in range(begin, end):
                    last = v.copy_predicated(quant[:, m, :], masks[:, r % 2, :], val_ps[:, r:r + 1].broadcast_to([P, D]))
                    if r + 1 < KEEP:
                        last = v.tensor_scalar(masks[:, (r + 1) % 2, :], norm[:, m, :], steps[:, r + 1:r + 2], None,
                                               ALU.is_le)
                    link(last)

            def further_steps(m):
                with dve.If(steps_n > KEEP):
                    with dve.Fori(KEEP, NC) as r:
                        v.tensor_copy(one_step[:, 0:1], steps[:, bass.ds(r, 1)])
                        settle(v.tensor_copy(one_step[:, 1:2], step_cb[:, bass.ds(r, 1)]))
                        settle(v.tensor_scalar(more_mask, norm[:, m, :], one_step[:, 0:1], None, ALU.is_le))
                        settle(v.copy_predicated(quant[:, m, :], more_mask, one_step[:, 1:2].broadcast_to([P, D])))

            def tail(m):
                q, n = quant[:, m, :], norm[:, m, :]
                if m in TAIL_ON_POOL:
                    v.nop().then_inc(quant_ready, 1)
                    return
                link(v.tensor_tensor(q, q, n, ALU.subtract))
                link(v.tensor_tensor(q, q, n, ALU.add))
                for k in range(K):
                    cols = q[:, k * P:(k + 1) * P]
                    last = v.scalar_tensor_tensor(cols, cols, scale[:, m, k:k + 1], delta[:, m, k * P:(k + 1) * P],
                                                  ALU.mult, ALU.add)
                last.then_inc(weff_dve, 1)

            def w0_low(m):
                dve.wait_ge(w0_hi_ready, m + 1)
                if m >= 2:
                    dve.wait_ge(l0_done, CHUNKS * (m - 1))
                v.tensor_tensor(w0_lo[:, m % 2, :], ps_w[:, :], w0_hi[:, m % 2, :].bitcast(F32),
                                ALU.subtract).then_inc(w0_ready, 1)

            for m in range(K):
                if m == 0:
                    add_delta(0)
                    add_delta(1)
                    dve.wait_ge(scale_ready, 2)
                first_step(m)
                if m == 0:
                    kept_steps(m, 0, KEEP)
                else:
                    part = KEEP - 2 if m - 1 in TAIL_ON_POOL else 2
                    kept_steps(m, 0, part)
                    w0_low(m - 1)
                    kept_steps(m, part, KEEP)
                further_steps(m)
                tail(m)
                if m == 0:
                    add_delta(2)
                    add_delta(3)

            def eye(a):
                dve.wait_ge(raw_in[a % RAW], 16 * (a // RAW + 1))
                add_eye(v, a).then_inc(eye_dve, 1)

            eye(ON_DVE[0])
            w0_low(K - 1)
            dve.wait_ge(slots_ps, 1)
            twos = batch_ps.rearrange("p (n s) -> p n s", s=2)
            link(v.tensor_scalar(batch_f[:, :], twos[:, :, 0], float(B + 1), float((B + 2) * B), ALU.mult, ALU.add))
            v.tensor_tensor(batch_i[:, :], batch_f[:, :], twos[:, :, 1], ALU.add).then_inc(batches_ready, 1)
            for a in ON_DVE:
                if a + 1 in ON_DVE:
                    eye(a + 1)
                dve.wait_ge(w_hi_ready, a + 1)
                w_low(v, a).then_inc(split_dve, 1)

            def place(parts, at, j):
                return parts[:, at, :].rearrange("p o (k q s) -> p (o k) q s", k=K, s=S)[:, :, j, :]

            def batch_of(b):
                return x1[:, bass.ds(b * BLK, BLK)].rearrange("p (k s) -> p k s", s=S)

            dve.wait_ge(batches_ready, 1)
            dve.wait_ge(tables_ready, 1)
            pairs_n = dve.value_load(pairs_i[0:1, 0:1], min_val=B // TB // 2, max_val=MAX_TILES // 2)
            dve.wait_ge(x1_ready, CHUNKS * K)
            with dve.Fori(0, pairs_n) as i:
                batches = load_batches(dve, i)
                for h in range(2):
                    t = 2 * i + h
                    dve.wait_ge(tiles_done, t + 1)
                    at = bass.ds(t % TILE_BUFS, 1)
                    for j, b in enumerate(batches[h]):
                        v.tensor_copy(place(tile_hi, at, j), batch_of(b)).then_inc(tile_hi_ready, 1)
                    dve.wait_ge(tile_hi_ready, TB * t + TB)
                    for j, b in enumerate(batches[h]):
                        hi = place(tile_hi, at, j)
                        v.tensor_tensor(place(tile_lo, at, j), batch_of(b), hi.bitcast(F32),
                                        ALU.subtract).then_inc(tile_ready, 1)

        @block.tensor
        def _(pe):
            mm = nc.tensor.matmul
            pe.nop().then_inc(tiles_done, TILE_BUFS)

            def lora(m):
                if m >= 2:
                    pe.wait_ge(delta_ready, m - 1)
                mm(ps_d[:, m % 2, :], lb[:, m * P:(m + 1) * P], la, start=True, stop=True).then_inc(delta_ps, 1)

            def turn(m):
                if m in TAIL_ON_POOL:
                    pe.wait_ge(weff_pool, TAIL_ON_POOL.index(m) + 1)
                else:
                    pe.wait_ge(weff_dve, 1 if m == 0 else K - len(TAIL_ON_POOL))
                if m >= 1:
                    pe.wait_ge(w0_ready, m)
                for k in range(K):
                    to = ps_w[:, k * P:(k + 1) * P]
                    last = mm(to, quant[:, m, k * P:(k + 1) * P], ident[:, :], start=True, stop=(k != m))
                    if k == m:
                        last = mm(to, ident[:, :], ident[:, :], start=False, stop=True)
                last.then_inc(turned_ready, 1)

            def layer0(m):
                pe.wait_ge(w0_ready, m + 1)
                parts = ((w0_hi, 0), (w0_lo, 0), (w0_hi, ROW))
                with pe.Fori(0, CHUNKS) as c:
                    if m == 0:
                        pe.wait_ge(x_ready, c + 1)
                    else:
                        pe.wait_ge(x1_ready, c + (CHUNKS * (m - 1) + 1))
                    for n, (w, low) in enumerate(parts):
                        for k in range(K):
                            cols = pairs[:, bass.ds(c * (2 * ROW) + (FIRST * 2 * ROW + low), ROW)].rearrange("p (q k s) -> p q k s", k=K, s=S)
                            last = mm(ps0[:, bass.ds(c, 1), :].rearrange("p c n -> p (c n)"),
                                      w[:, m % 2, k * P:(k + 1) * P], cols[:, :, k, :],
                                      start=(n == 0 and k == 0), stop=(n == 2 and k == K - 1))
                    last.then_inc(l0_done, 1)

            pe.wait_ge(lora_in, 32)
            lora(0)
            pe.wait_ge(members_ready, 1)
            mm(counts_ps[:, 0, :], ones[:, :], is_adapter[:, :], start=True, stop=True)
            mm(counts_ps[:, 1, :], earlier[:, :], is_adapter[:, :], start=True, stop=True).then_inc(counts_ps_ready, 1)
            for m in range(1, K):
                lora(m)
            pe.wait_ge(ident_ready, 1)
            for m in range(K):
                turn(m)
                layer0(m)
                if m == K - 2:
                    pe.wait_ge(slots_ready, 1)
                    pe.wait_ge(delta_ready, K)
                    mm(batch_ps, i_col_b[0:B, :], at_slot[:, :], start=True, stop=True).then_inc(slots_ps, 1)

            pe.wait_ge(tables_ready, 1)
            pairs_n = pe.value_load(pairs_i[0:1, 0:1], min_val=B // TB // 2, max_val=MAX_TILES // 2)

            def some_tiles(i, n):
                of_tiles = load_values(pe, tile_i[0:1, bass.ds(TILE_BUFS * i, n)], 0, RING * NA - 1)
                for h in range(n):
                    t = TILE_BUFS * i + h
                    pe.wait_ge(tile_ready, TB * t + TB)
                    pe.wait_ge(split_pool, of_tiles[h] // RING + 1)
                    pe.wait_ge(y_ready, t + 1)
                    at = of_tiles[h] % RING * (2 * ROW)
                    parts = ((tile_hi, 0), (tile_lo, 0), (tile_hi, ROW))
                    for n, (xs, low) in enumerate(parts):
                        for k in range(K):
                            last = mm(ps_y[:, h, :], xs[:, h, k * P:(k + 1) * P],
                                      pairs[:, bass.ds(at + (low + k * D), D)],
                                      start=(n == 0 and k == 0), stop=(n == 2 and k == K - 1))
                    last.then_inc(tiles_done, 1)

            assert TILE_BUFS == YB == 4
            quads_n = pairs_n // 2
            with pe.Fori(0, quads_n) as i:
                some_tiles(i, TILE_BUFS)
            with pe.If(pairs_n > quads_n * 2):
                some_tiles(quads_n, 2)


def kernel(x, condB_codebook, itok_B_0_15, L0_cond_weight, L0_cond_scale_log, L0_cond_lora_A, L0_cond_lora_B,
           L1_cond_weight):
    import numpy as np
    import concourse.bacc as bacc
    from concourse.bass_utils import run_bass_kernel_spmd as run

    arrays = {
        "x_t": x.reshape(B, S, K, P).transpose(0, 3, 2, 1).reshape(B, P, BLK),
        "codebook": condB_codebook,
        "ids": itok_B_0_15,
        "w0": L0_cond_weight,
        "scales": L0_cond_scale_log.reshape(K, P, K).transpose(1, 0, 2),
        "lora_a": L0_cond_lora_A,
        "lora_bt": L0_cond_lora_B.T,
        "w1_t": L1_cond_weight.reshape(NA, D, K, P).transpose(0, 3, 2, 1).reshape(NA, P, ROW),
    }
    arrays = {name: np.ascontiguousarray(a) for name, a in arrays.items()}
    nc = bacc.Bacc("TRN2", target_bir_lowering=False, num_devices=1)
    args = [nc.dram_tensor(name, a.shape, mybir.dt.from_np(a.dtype), kind="ExternalInput").ap()
            for name, a in arrays.items()]
    out = nc.dram_tensor("result", (B, S, D), F32, kind="ExternalOutput").ap()
    adapter_mlp(nc, *args, out)
    return run(nc, [arrays], core_ids=[0]).results[0]["result"]
```

```python
from contextlib import ExitStack

import concourse.bass as bass
from concourse import mybir

F32 = mybir.dt.float32
F32R = mybir.dt.float32r
I32 = mybir.dt.int32
U8 = mybir.dt.uint8
ALU = mybir.AluOpType
ACT = mybir.ActivationFunctionType
AX = mybir.AxisListType.X

P = 128
B = 64
S = 32
D = 512
K = D // P
NA = 16
RANK = 64
NC = 64
LEVELS = 6
TB = P // S
MAX_TILES = NA + (B - NA) // TB
CHUNKS = 4
CB = B // CHUNKS
BLK = K * S
ROW = K * D
RAW = 3
RING = 6
FIRST = 2
ON_DVE = (2, 3, 4)
assert ON_DVE == tuple(range(ON_DVE[0], ON_DVE[-1] + 1))
ON_POOL = tuple(a for a in range(NA) if a not in ON_DVE)
TILE_BUFS = 4
YB = 4
POOL_MASKS = {0: (5, 7), 2: (4, 5, 6, 7), 3: (0, 1, 2, 3)}
TURN_STEPS = {1: 1, 2: 1, 3: 3}
W_HIGH_AFTER = (0, 2, 3, 4, 6, 7, 8, 9, 10, 11)
assert all(before >= n for n, before in enumerate(W_HIGH_AFTER))
ROUND = float(2 ** 23)
KEEP = 8
BIG = 3.0e38


def adapter_mlp(nc, x, codebook, ids, w0, scales, lora_a, lora_bt, w1, out):
    ctx = ExitStack()
    with ctx:
        def sb(name, shape, dt=F32):
            return ctx.enter_context(nc.sbuf_tensor(name, shape, dt))

        def sem(name):
            return ctx.enter_context(nc.semaphore(name))

        x1 = sb("x1", [P, (B + 1) * BLK])
        pairs = sb("pairs", [P, RING * 2 * ROW], F32R)
        assert FIRST + CHUNKS == RING and CB * BLK == ROW and BLK == 2 * B
        raw = sb("raw", [P, RAW, ROW])
        w0_sb = sb("w0_sb", [P, K, D])
        norm = w0_sb
        scale_log = sb("scale_log", [P, K, K])
        scale = sb("scale", [P, K, K])
        inv_scale = sb("inv_scale", [P, K, K])
        delta = sb("delta", [P, K, D])
        y = sb("y", [P, YB, D])
        quant = y
        assert K == YB
        la, lb = y[0:RANK, 1, :], y[0:RANK, 2, :]
        masks = sb("masks", [P, 2, D], U8)
        tile_hi = sb("tile_hi", [P, TILE_BUFS, D], F32R)
        tile_lo = sb("tile_lo", [P, TILE_BUFS, D], F32R)
        w0_hi, w0_lo = tile_hi[:, 2:4, :], tile_lo[:, 2:4, :]
        ident = sb("ident", [P, P])
        cbk = sb("cbk", [P, NC])
        cb = sb("cb", [P, NC])
        cmax = sb("cmax", [P, 2])
        thr = sb("thr", [P, NC])
        upper = sb("upper", [P, NC])
        lower = sb("lower", [P, NC])
        key = sb("key", [P, NC])
        key2 = sb("key2", [P, NC])
        scratch = sb("scratch", [1, MAX_TILES * NA + 3 * MAX_TILES])
        hit = quant[:, K - 1, :].rearrange("p (r n) -> p r n", r=KEEP)
        steps = sb("steps", [P, NC])
        step_cb = sb("step_cb", [P, NC])
        pool_masks = sb("pool_masks", [P, KEEP, D], U8)
        more_mask = masks[:, 0, :]
        found = sb("found", [P, KEEP])
        found_cb = sb("found_cb", [P, KEEP])
        one_step = sb("one_step", [P, 2])
        odd = sb("odd", [1, 16])
        is_adapter = sb("is_adapter", [B, NA])
        n_steps = sb("n_steps", [P, 1])
        n_steps_i = sb("n_steps_i", [P, 1], I32)
        id_col_i = sb("id_col_i", [B, 1], I32)
        id_col = sb("id_col", [B, 1])
        ones = sb("ones", [B, B])
        earlier = sb("earlier", [B, B])
        counts = sb("counts", [B, 2, NA])
        tiles = sb("tiles", [B, NA])
        tile_end = sb("tile_end", [B, 2, NA])
        tile_beg = sb("tile_beg", [B, NA])
        beg_of = sb("beg_of", [B, NA])
        slot = sb("slot", [B, 1])
        before = scratch[0:1, 0:MAX_TILES * NA].rearrange("p (t a) -> p t a", a=NA)
        adapter = sb("adapter", [1, MAX_TILES])
        adapter_part = scratch[0:1, MAX_TILES * NA:].rearrange("p (n t) -> p n t", n=3)
        tile_i = sb("tile_i", [1, MAX_TILES + 2], I32)
        end_i = sb("end_i", [1, NA], I32)
        pairs_f = sb("pairs_f", [1, 1])
        pairs_i = sb("pairs_i", [1, 1], I32)
        batch_f = sb("batch_f", [1, MAX_TILES * TB // 2])
        batch_i = sb("batch_i", [1, (MAX_TILES + 2) * TB // 2], I32)
        x1_at_i = sb("x1_at_i", [1, (MAX_TILES + 2) * TB], I32)
        i_row = sb("i_row", [P, NC])
        i_col_b = sb("i_col_b", [P, 1])
        i_slot = sb("i_slot", [B, MAX_TILES * TB])
        at_slot = i_slot
        i_tile = sb("i_tile", [1, MAX_TILES])

        ps0 = ctx.enter_context(nc.psum_tensor("ps0", [P, CHUNKS, D], F32))
        ps_y = ps0
        assert CHUNKS == YB
        ps_d = ctx.enter_context(nc.psum_tensor("ps_d", [P, 2, D], F32))
        ps_w = ctx.enter_context(nc.psum_tensor("ps_w", [P, D], F32))
        ps_v = ctx.enter_context(nc.psum_tensor("ps_v", [P, D], F32))
        val_ps = ps_v[:, 0:KEEP]
        counts_ps = ps_w[0:B, 0:2 * NA].rearrange("p (n a) -> p n a", n=2)
        batch_ps = ps_d[0:1, 0, 0:MAX_TILES * TB]

        ids_in, cb_in, lora_in = (sem(n) for n in ("ids_in", "cb_in", "lora_in"))
        w0_in = [sem(f"w0_in{i}") for i in range(2)]
        slog_in = sem("slog_in")
        x_in = [sem(f"x_in{c}") for c in range(CHUNKS)]
        raw_in = [sem(f"raw_in{r}") for r in range(RAW)]
        consts = sem("consts")
        pool_step = sem("pool_step")
        ident_ready = sem("ident_ready")
        dve_step = sem("dve_step")
        members_ready = sem("members_ready")
        counts_ps_ready = sem("counts_ps_ready")
        counts_ready = sem("counts_ready")
        slots_ready = sem("slots_ready")
        slots_ps = sem("slots_ps")
        tables_ready = sem("tables_ready")
        batches_ready = sem("batches_ready")
        scale_ready = sem("scale_ready")
        delta_ps = sem("delta_ps")
        delta_ready = sem("delta_ready")
        sum_ready = sem("sum_ready")
        norm_ready = sem("norm_ready")
        first_norm = sem("first_norm")
        masks_ready = sem("masks_ready")
        weff_ready = sem("weff_ready")
        turned_ready = sem("turned_ready")
        w0_hi_ready = sem("w0_hi_ready")
        w0_ready = sem("w0_ready")
        x_hi_ready = sem("x_hi_ready")
        x_ready = sem("x_ready")
        l0_done = sem("l0_done")
        x1_ready = sem("x1_ready")
        eye_pool = sem("eye_pool")
        eye_dve = sem("eye_dve")
        w_hi_ready = sem("w_hi_ready")
        split_pool = sem("split_pool")
        split_dve = sem("split_dve")
        tile_hi_ready = sem("tile_hi_ready")
        tile_ready = sem("tile_ready")
        tiles_done = sem("tiles_done")
        y_ready = sem("y_ready")
        y_free = sem("y_free")
        all_stored = sem("all_stored")
        stored = [sem(f"stored{i}") for i in range(2)]

        def ring_slot(a):
            at = a % RING * 2 * ROW
            return pairs[:, at:at + ROW], pairs[:, at + ROW:at + 2 * ROW]

        def wait_for(eng, a, on_pool, on_dve):
            if a in ON_POOL:
                eng.wait_ge(on_pool, ON_POOL.index(a) + 1)
            else:
                eng.wait_ge(on_dve, ON_DVE.index(a) + 1)

        def add_eye(engine, a):
            r = raw[:, a % RAW, :]
            d = bass.AP(r.tensor, r.offset, [list(r.ap[0]), [D + P, K], [1, P]])
            eye = ident[:, :].rearrange("p (o n) -> p o n", o=1).broadcast_to([P, K, P])
            return engine.tensor_tensor(d, d, eye, ALU.add)

        def w_low(engine, a):
            hi, lo = ring_slot(a)
            return engine.tensor_tensor(lo, raw[:, a % RAW, :], hi.bitcast(F32), ALU.subtract)

        def load_values(eng, at, least, most):
            return nc.values_load_multi_w_load_instructions(at, engines=[eng.engine], min_val=least, max_val=most)[1]

        block = ctx.enter_context(nc.Block())

        @block.sync
        def _(sp):
            w0_blocks = w0.rearrange("(m p) n -> p m n", p=P)
            sp.dma_start(cbk[:, :], codebook.rearrange("(a n) -> a n", a=1).broadcast_to([P, NC])).then_inc(cb_in, 16)
            sp.dma_start(scale_log[:, :, :], scales).then_inc(slog_in, 16)
            sp.dma_start(w0_sb[:, 0, :], w0_blocks[:, 0, :]).then_inc(w0_in[0], 16)
            for c in range(CHUNKS):
                sp.dma_start(x1[:, c * ROW:(c + 1) * ROW].rearrange("p (q n) -> p q n", n=BLK),
                             x[c * CB:(c + 1) * CB].rearrange("q p n -> p q n")).then_inc(x_in[c], 16)
                if c == 0:
                    sp.dma_start(w0_sb[:, 1:, :], w0_blocks[:, 1:, :]).then_inc(w0_in[1], 16)
            assert YB == 4
            sp.sem_inc(y_free, 2)
            for h in range(2):
                sp.sem_inc(stored[h], 1)
            sp.wait_ge(tables_ready, 1)
            sp.wait_ge(batches_ready, 1)
            pairs_n = sp.value_load(pairs_i[0:1, 0:1], min_val=B // TB // 2, max_val=MAX_TILES // 2)
            quads_n = pairs_n // 2

            def some_tiles(i, n):
                twos = load_values(sp, batch_i[0:1, bass.ds(i * (YB * TB // 2), n * TB // 2)], 0, (2 * B + 1) * B)
                to = [nc.snap(b, engines=[sp.engine]) for two in twos for b in (two // (2 * B), two % (2 * B))]
                for h in range(n):
                    sp.wait_ge(y_ready, YB * i + (h + YB + 1))
                    for j, b in enumerate(to[h * TB:(h + 1) * TB]):
                        to_b = nc.s_assert_within(b, 0, B - 1, skip_runtime_bounds_check_because="else not stored")
                        sp.dma_start(out[bass.ds(to_b, 1)].rearrange("b s n -> (b s) n"),
                                     y[S * j:S * j + S, h, :], cond=b < B).then_inc(stored[h // 2], 16)
                    if h == 0:
                        sp.wait_ge(stored[1], i * (2 * 16 * TB) + 1)
                        sp.sem_inc(y_free, 2)
                    if h == 2:
                        sp.wait_ge(stored[0], i * (2 * 16 * TB) + (2 * 16 * TB + 1))
                        sp.sem_inc(y_free, 2)

            with sp.Fori(0, quads_n) as i:
                some_tiles(i, YB)
            with sp.If(pairs_n > quads_n * 2):
                some_tiles(quads_n, 2)
            sp.wait_ge(stored[0], (pairs_n + 1) // 2 * (2 * 16 * TB) + 1)
            sp.wait_ge(stored[1], quads_n * (2 * 16 * TB) + 1)
            sp.sem_inc(all_stored, 1)

        @block.gpsimd
        def _(pool):
            g = nc.gpsimd
            made = [0]

            def link(ins):
                made[0] += 1
                ins.then_inc(pool_step, 1)
                pool.wait_ge(pool_step, made[0])

            def iota(t, pattern, cm=0, base=0):
                g.iota(t, pattern=pattern, base=base, channel_multiplier=cm,
                       allow_small_or_imprecise_dtypes=True).then_inc(consts, 1)

            pool.dma_start(id_col_i[:, :], ids.rearrange("(n a) -> n a", a=1)).then_inc(ids_in, 16)
            link(g.memset(ident[:, :], 0.0))
            g.affine_select(out=ident[:, :], in_=ident[:, :], compare_op=ALU.not_equal, fill=1.0, base=0,
                            pattern=[[-1, P]], channel_multiplier=1).then_inc(ident_ready, 1)
            g.memset(x1[:, B * BLK:], 0.0).then_inc(consts, 1)
            iota(i_row[:, :], [[1, NC]])
            iota(i_col_b[:, :], [[0, 1]], cm=1, base=-B)
            iota(i_slot[:, :], [[1, MAX_TILES * TB]])
            iota(i_tile[:, :], [[1, MAX_TILES]])
            g.memset(ones[:, :], 1.0).then_inc(consts, 1)
            pool.wait_ge(consts, 6)
            g.affine_select(out=earlier[:, :], in_=ones[:, :], compare_op=ALU.is_gt, fill=0.0, base=0,
                            pattern=[[1, B]], channel_multiplier=-1).then_inc(consts, 1)

            def x_low(c):
                hi, lo = ring_slot(FIRST + c)
                pool.wait_ge(x_hi_ready, c + 1)
                g.tensor_tensor(lo, x1[:, c * ROW:(c + 1) * ROW], hi.bitcast(F32), ALU.subtract).then_inc(x_ready, 1)

            def steps_masks(m):
                for r in POOL_MASKS[m]:
                    last = g.tensor_scalar(pool_masks[:, r, :], norm[:, m, :], steps[:, r:r + 1], None, ALU.is_le)
                last.then_inc(masks_ready, 1)

            def compare(to, a, b, op):
                link(g.tensor_tensor(to, a, b, ALU.subtract))
                link(g.tensor_scalar(to, to, 0.0, None, op))

            def total(to, of, n):
                while n > 2:
                    n //= 2
                    link(g.tensor_tensor(of[:, :, 0:n], of[:, :, 0:n], of[:, :, n:2 * n], ALU.add))
                link(g.tensor_tensor(to.rearrange("p (r o) -> p r o", o=1), of[:, :, 0:1], of[:, :, 1:2], ALU.add))

            def tables():
                pool.wait_ge(ids_in, 16)
                link(g.tensor_copy(id_col[:, :], id_col_i[:, :]))
                pool.wait_ge(consts, 7)
                g.tensor_scalar(is_adapter[:, :], i_row[0:B, 0:NA], id_col[:, 0:1], None,
                                ALU.is_equal).then_inc(members_ready, 1)
                pool.wait_ge(members_ready, 1)
                pool.wait_ge(counts_ready, 1)
                assert TB == 4
                link(g.tensor_scalar(tiles[:, :], counts[:, 0, :], 1.0 / TB, 0.375, ALU.mult, ALU.add))
                link(g.tensor_scalar(tiles[:, :], tiles[:, :], ROUND, None, ALU.add))
                link(g.tensor_scalar(tiles[:, :], tiles[:, :], -ROUND, None, ALU.add))
                assert NA == 16
                src = tiles[:, :]
                for n, d in enumerate((1, 2, 4, 8)):
                    dst = tile_end[:, n % 2, :]
                    g.tensor_copy(dst[:, 0:d], src[:, 0:d])
                    link(g.tensor_tensor(dst[:, d:], src[:, d:], src[:, 0:NA - d], ALU.add))
                    src = dst
                ends = src
                g.tensor_scalar(end_i[:, 0:NA - 1], ends[0:1, 0:NA - 1], 1.0, None, ALU.add)
                link(g.tensor_tensor(tile_beg[:, :], ends, tiles[:, :], ALU.subtract))
                link(g.tensor_scalar(tile_beg[:, :], tile_beg[:, :], float(TB), None, ALU.mult))
                link(g.tensor_tensor(tile_beg[:, :], tile_beg[:, :], counts[:, 1, :], ALU.add))
                link(g.tensor_tensor(beg_of[:, :], is_adapter[:, :], tile_beg[:, :], ALU.mult))
                total(slot[:, :], beg_of[:, :].rearrange("p (o n) -> p o n", o=1), NA)
                g.tensor_scalar(at_slot[:, :], i_slot[:, :], slot[:, 0:1], None, ALU.is_equal).then_inc(slots_ready, 1)
                return ends

            def tile_tables(ends):
                compare(before, ends[0:1, :].rearrange("p (o n) -> p o n", o=1).broadcast_to([1, MAX_TILES, NA]),
                        i_tile[:, :].rearrange("p (t o) -> p t o", o=1).broadcast_to([1, MAX_TILES, NA]),
                        ALU.is_le)
                total(adapter[:, :], before, NA)
                link(g.tensor_scalar(adapter[:, :], adapter[:, :], float(NA - 1), None, ALU.min))
                own = ON_DVE[0]
                part = adapter_part
                g.tensor_scalar(part[:, 0, :], adapter[:, :], float(own - 1), None, ALU.min)
                g.tensor_scalar(part[:, 1, :], adapter[:, :], -float(ON_DVE[-1]), 0.0, ALU.add, ALU.max)
                assert 2 * RING < NA <= 3 * RING
                link(g.tensor_scalar(part[:, 2, :], adapter[:, :], float(RING), -float(RING), ALU.is_ge, ALU.mult))
                g.tensor_tensor(part[:, 0, :], part[:, 0, :], part[:, 1, :], ALU.add)
                link(g.tensor_tensor(part[:, 2, :], part[:, 2, :], adapter[:, :], ALU.add))
                link(g.tensor_scalar(adapter[:, :], adapter[:, :], float(2 * RING), -float(RING), ALU.is_ge, ALU.mult))
                link(g.tensor_tensor(part[:, 2, :], part[:, 2, :], adapter[:, :], ALU.add))
                link(g.tensor_scalar(part[:, 0, :], part[:, 0, :], float(RING), None, ALU.mult))
                link(g.tensor_tensor(part[:, 0, :], part[:, 0, :], part[:, 2, :], ALU.add))
                g.tensor_copy(tile_i[:, 0:MAX_TILES], part[:, 0, :])
                ODD = 16
                link(g.tensor_scalar(odd[:, :], i_tile[:, 0:ODD], 2.0, 1.0, ALU.mult, ALU.add))
                compare(odd[:, :], odd[:, :], ends[0:1, NA - 1:NA].broadcast_to([1, ODD]), ALU.is_le)
                total(pairs_f[:, :], odd[:, :].rearrange("p (o n) -> p o n", o=1), ODD)
                g.tensor_scalar(end_i[:, NA - 1:NA], pairs_f[:, :], 2.0, 1.0, ALU.mult, ALU.add)
                g.tensor_copy(pairs_i[:, :], pairs_f[:, :]).then_inc(tables_ready, 1)

            def eye(a):
                pool.wait_ge(raw_in[a % RAW], 16 * (a // RAW + 1))
                add_eye(g, a).then_inc(eye_pool, 1)

            def split(a):
                pool.wait_ge(w_hi_ready, a + 1)
                w_low(g, a).then_inc(split_pool, 1)

            ends = tables()
            pool.wait_ge(first_norm, 1)
            steps_masks(0)
            for c in range(CHUNKS):
                x_low(c)
            for m in (2, 3):
                pool.wait_ge(norm_ready, m)
                steps_masks(m)
            tile_tables(ends)
            pool.wait_ge(ident_ready, 1)
            eye(0)
            eye(1)
            split(0)
            split(1)
            rest = [a for a in ON_POOL if a > 1]
            eye(rest[0])
            for a, following in zip(rest, rest[1:]):
                eye(following)
                split(a)
            split(rest[-1])

        @block.scalar
        def _(act):
            activation = nc.scalar.activation
            act.dma_start(la, lora_a).then_inc(lora_in, 16)
            act.dma_start(lb, lora_bt).then_inc(lora_in, 16)

            def load_w(a):
                if a >= RAW:
                    wait_for(act, a - RAW, split_pool, split_dve)
                act.dma_start(raw[:, a % RAW, :], w1[a]).then_inc(raw_in[a % RAW], 16)

            def delta_out(m):
                act.wait_ge(delta_ps, m + 1)
                activation(delta[:, m, :], ps_d[:, m % 2, :], ACT.Copy, scale=0.5).then_inc(delta_ready, 1)

            def normalise(m):
                act.wait_ge(sum_ready, m + 1)
                for k in range(K):
                    cols = norm[:, m, k * P:(k + 1) * P]
                    last = activation(cols, cols, ACT.Copy, scale=inv_scale[:, m, k:k + 1])
                last.then_inc(norm_ready, 1)

            def x_high(c):
                act.wait_ge(x_in[c], 16)
                activation(ring_slot(FIRST + c)[0], x1[:, c * ROW:(c + 1) * ROW], ACT.Copy).then_inc(x_hi_ready, 1)

            def w0_high(m):
                act.wait_ge(turned_ready, m + 1)
                if m >= 2:
                    act.wait_ge(l0_done, CHUNKS * (m - 1))
                activation(w0_hi[:, m % 2, :], ps_w[:, :], ACT.Copy).then_inc(w0_hi_ready, 1)

            def x1_out(m, c):
                to = x1[:, bass.ds(c * ROW, ROW)].rearrange("p (q k s) -> p q k s", k=K, s=S)[:, :, m, :]
                activation(to, ps0[:, bass.ds(c, 1), :].rearrange("p c (q s) -> p (c q) s", s=S),
                           ACT.Copy).then_inc(x1_ready, 1)

            def x1_block(m):
                with act.Fori(0, CHUNKS - 1) as c:
                    act.wait_ge(l0_done, c + (CHUNKS * m + 1))
                    x1_out(m, c)
                w0_high(m + 1)
                act.wait_ge(l0_done, CHUNKS * (m + 1))
                x1_out(m, CHUNKS - 1)

            def w_high(a):
                wait_for(act, a, eye_pool, eye_dve)
                activation(ring_slot(a)[0], raw[:, a % RAW, :], ACT.Copy).then_inc(w_hi_ready, 1)

            def result(t1):
                act.wait_ge(tiles_done, t1 + TILE_BUFS)
                act.wait_ge(y_free, t1)
                at = bass.ds((t1 + (YB - 1)) % YB, 1)
                activation(y[:, at, :], ps_y[:, at, :], ACT.Copy).then_inc(y_ready, 1)

            act.wait_ge(slog_in, 16)
            activation(inv_scale[:, :, :], scale_log[:, :, :], ACT.Exp, scale=-1.0).then_inc(scale_ready, 1)
            activation(scale[:, :, :], scale_log[:, :, :], ACT.Exp).then_inc(scale_ready, 1)
            act.wait_ge(scale_ready, 2)
            delta_out(0)
            act.wait_ge(counts_ps_ready, 1)
            activation(counts[:, :, :], counts_ps, ACT.Copy).then_inc(counts_ready, 1)
            delta_out(1)
            delta_out(2)
            delta_out(3)
            x_high(0)
            normalise(1)
            for a in range(RAW):
                load_w(a)
            for c in range(1, CHUNKS):
                x_high(c)
            w0_high(0)
            normalise(2)
            normalise(3)
            x1_block(0)
            x1_block(1)
            w_high(0)
            w_high(1)
            x1_block(2)
            load_w(3)
            load_w(4)
            for c in range(CHUNKS):
                act.wait_ge(l0_done, CHUNKS * (K - 1) + c + 1)
                x1_out(K - 1, c)
                if c == 2:
                    load_w(5)
                if c < CHUNKS - 1:
                    w_high(FIRST + c)
            act.sem_inc(y_ready, YB)
            load_w(RING)
            load_w(RING + 1)
            act.wait_ge(tables_ready, 1)
            begin = 1
            w_high(RING - 1)
            for a in range(NA):
                end = act.value_load(end_i[0:1, a:a + 1], min_val=1, max_val=MAX_TILES + 1)
                with act.If(end > begin):
                    with act.Fori(begin, end) as t1:
                        result(t1)
                begin = end
                for coming in range(RING, NA):
                    if W_HIGH_AFTER[coming - RING] == a:
                        w_high(coming)
                        if coming + 2 < NA:
                            load_w(coming + 2)

        @block.vector
        def _(dve):
            made = [0]

            def link(ins):
                made[0] += 1
                ins.then_inc(dve_step, 1)
                dve.wait_ge(dve_step, made[0])

            v = nc.vector
            v.memset(upper[:, :], BIG)
            v.memset(lower[:, :], -BIG)
            dve.wait_ge(cb_in, 16)
            link(v.tensor_reduce(cmax[:, 0:1], cbk[:, :], AX, ALU.max, apply_absolute_value=True))
            link(v.tensor_scalar(cmax[:, 1:2], cmax[:, 0:1], 1e-8, None, ALU.max))
            link(v.reciprocal(cmax[:, 0:1], cmax[:, 1:2]))
            link(v.tensor_scalar(cb[:, :], cbk[:, :], cmax[:, 0:1], None, ALU.mult))
            link(v.tensor_tensor(thr[:, 0:NC - 1], cb[:, 0:NC - 1], cb[:, 1:NC], ALU.add))
            link(v.tensor_scalar(thr[:, 0:NC - 1], thr[:, 0:NC - 1], 0.5, None, ALU.mult))
            for level in range(LEVELS):
                nodes, half = 1 << level, NC >> (level + 1)
                up = upper[:, :].rearrange("p (n s h) -> p n s h", s=2, h=half)[:, :, 0, :]
                lo = lower[:, :].rearrange("p (n s h) -> p n s h", s=2, h=half)[:, :, 1, :]
                mid = thr[:, half - 1:NC - 1:2 * half]
                mid = mid.rearrange("p (n o) -> p n o", o=1).broadcast_to([P, nodes, half])
                v.tensor_tensor(up, up, mid, ALU.min)
                link(v.tensor_tensor(lo, lo, mid, ALU.max))
            link(v.tensor_tensor(key2[:, :], lower[:, :], upper[:, :], ALU.is_lt))
            link(v.memset(key2[:, NC - 1:NC], 0.0))
            link(v.tensor_tensor(key[:, :], key2[:, :], upper[:, :], ALU.mult))
            v.tensor_reduce(n_steps[:, :], key2[:, :], AX, ALU.add)
            link(v.tensor_scalar(key2[:, :], key2[:, :], BIG, BIG, ALU.mult, ALU.subtract))
            link(v.tensor_tensor(key[:, :], key[:, :], key2[:, :], ALU.add))
            v.tensor_copy(n_steps_i[:, :], n_steps[:, :])
            link(v.max(steps[:, 0:KEEP], key[:, :]))
            for r in range(KEEP):
                last = v.scalar_tensor_tensor(hit[:, r, :], key[:, :], steps[:, r:r + 1], cb[:, :], ALU.is_equal,
                                              ALU.mult, accum_out=step_cb[:, r:r + 1])
            link(last)
            link(v.tensor_copy(val_ps, step_cb[:, 0:KEEP]))

            def all_hits(at):
                settle(v.tensor_tensor(hit[:, :, :], key[:, :].rearrange("p (o n) -> p o n", o=1).broadcast_to([P, KEEP, NC]),
                                       at.rearrange("p (r o) -> p r o", o=1).broadcast_to([P, KEEP, NC]), ALU.is_equal))
                settle(v.tensor_tensor(hit[:, :, :], hit[:, :, :],
                                       cb[:, :].rearrange("p (o n) -> p o n", o=1).broadcast_to([P, KEEP, NC]), ALU.mult))

            def settle(ins):
                dve.drain()

            steps_n = dve.value_load(n_steps_i[0:1, 0:1], min_val=0, max_val=NC)
            with dve.If(steps_n > KEEP):
                v.tensor_copy(found[:, :], steps[:, 0:KEEP])
                settle(v.tensor_copy(key2[:, :], key[:, :]))
                with dve.Fori(1, NC // KEEP) as r:
                    settle(v.match_replace(key2[:, :], found[:, :], key2[:, :], -BIG))
                    settle(v.max(found[:, :], key2[:, :]))
                    all_hits(found[:, :])
                    settle(v.tensor_reduce(found_cb[:, :], hit[:, :, :], AX, ALU.add))
                    v.tensor_copy(steps[:, bass.ds(r * KEEP, KEEP)], found[:, :])
                    settle(v.tensor_copy(step_cb[:, bass.ds(r * KEEP, KEEP)], found_cb[:, :]))

            def add_delta(m):
                dve.wait_ge(delta_ready, m + 1)
                if m <= 1:
                    dve.wait_ge(w0_in[m], 16)
                v.tensor_tensor(norm[:, m, :], delta[:, m, :], w0_sb[:, m, :], ALU.add).then_inc(sum_ready, 1)

            def own_mask(m, r):
                if r < KEEP and r not in POOL_MASKS.get(m, ()):
                    return v.tensor_scalar(masks[:, r % 2, :], norm[:, m, :], steps[:, r:r + 1], None, ALU.is_le)

            def first_step(m):
                if m >= 1:
                    dve.wait_ge(norm_ready, m)
                copied = v.tensor_copy(quant[:, m, :], cb[:, NC - 1:NC].broadcast_to([P, D]))
                link(own_mask(m, 0) or copied)

            def kept_steps(m, begin, end):
                for r in range(begin, end):
                    mask = masks[:, r % 2, :]
                    if r in POOL_MASKS.get(m, ()):
                        dve.wait_ge(masks_ready, list(POOL_MASKS).index(m) + 1)
                        mask = pool_masks[:, r, :]
                    copied = v.copy_predicated(quant[:, m, :], mask, val_ps[:, r:r + 1].broadcast_to([P, D]))
                    link(own_mask(m, r + 1) or copied)

            def further_steps(m):
                with dve.If(steps_n > KEEP):
                    with dve.Fori(KEEP, NC) as r:
                        v.tensor_copy(one_step[:, 0:1], steps[:, bass.ds(r, 1)])
                        settle(v.tensor_copy(one_step[:, 1:2], step_cb[:, bass.ds(r, 1)]))
                        settle(v.tensor_scalar(more_mask, norm[:, m, :], one_step[:, 0:1], None, ALU.is_le))
                        settle(v.copy_predicated(quant[:, m, :], more_mask, one_step[:, 1:2].broadcast_to([P, D])))

            def tail(m):
                q, n = quant[:, m, :], norm[:, m, :]
                link(v.tensor_tensor(q, q, n, ALU.subtract))
                link(v.tensor_tensor(q, q, n, ALU.add))
                for k in range(K):
                    cols = q[:, k * P:(k + 1) * P]
                    last = v.scalar_tensor_tensor(cols, cols, scale[:, m, k:k + 1], delta[:, m, k * P:(k + 1) * P],
                                                  ALU.mult, ALU.add)
                last.then_inc(weff_ready, 1)

            def w0_low(m):
                dve.wait_ge(w0_hi_ready, m + 1)
                if m >= 2:
                    dve.wait_ge(l0_done, CHUNKS * (m - 1))
                v.tensor_tensor(w0_lo[:, m % 2, :], ps_w[:, :], w0_hi[:, m % 2, :].bitcast(F32),
                                ALU.subtract).then_inc(w0_ready, 1)

            for m in range(K):
                if m == 0:
                    add_delta(0)
                    dve.wait_ge(sum_ready, 1)
                    dve.wait_ge(scale_ready, 2)
                    for k in range(K):
                        cols = norm[:, 0, k * P:(k + 1) * P]
                        last = v.tensor_scalar(cols, cols, inv_scale[:, 0, k:k + 1], None, ALU.mult)
                    last.then_inc(first_norm, 1)
                    dve.wait_ge(first_norm, 1)
                    add_delta(1)
                first_step(m)
                if m == 0:
                    kept_steps(m, 0, KEEP)
                else:
                    kept_steps(m, 0, TURN_STEPS[m])
                    w0_low(m - 1)
                    kept_steps(m, TURN_STEPS[m], KEEP)
                further_steps(m)
                tail(m)
                if m == 0:
                    add_delta(2)
                    add_delta(3)

            def x1_batches(tile, n):
                return load_values(dve, x1_at_i[0:1, bass.ds(tile * TB, n * TB)], 0, B * BLK)

            def eye(a):
                dve.wait_ge(raw_in[a % RAW], 16 * (a // RAW + 1))
                add_eye(v, a).then_inc(eye_dve, 1)

            eye(ON_DVE[0])
            w0_low(K - 1)
            dve.wait_ge(slots_ps, 1)
            here = slice(0, MAX_TILES * TB)
            v.tensor_scalar(x1_at_i[:, here], batch_ps, float(BLK), float(B * BLK), ALU.mult, ALU.add)
            twos = batch_ps.rearrange("p (n s) -> p n s", s=2)
            link(v.tensor_scalar(batch_f[:, :], twos[:, :, 0], 2.0 * B, float((2 * B + 1) * B), ALU.mult, ALU.add))
            v.tensor_tensor(batch_i[:, 0:MAX_TILES * TB // 2], batch_f[:, :], twos[:, :, 1],
                            ALU.add).then_inc(batches_ready, 1)
            dve.wait_ge(batches_ready, 1)
            first_batches = x1_batches(0, TILE_BUFS)
            for a in ON_DVE:
                if a + 1 in ON_DVE:
                    eye(a + 1)
                dve.wait_ge(w_hi_ready, a + 1)
                w_low(v, a).then_inc(split_dve, 1)

            def place(parts, h, j):
                return parts[:, h, :].rearrange("p (k q s) -> p k q s", k=K, s=S)[:, :, j, :]

            def batch_at(b):
                return x1[:, bass.ds(b, BLK)].rearrange("p (k s) -> p k s", s=S)

            def some_tiles(i, n, batches):
                for h in range(n):
                    t = TILE_BUFS * i + h
                    dve.wait_ge(tiles_done, t + 1)
                    here = batches[h * TB:(h + 1) * TB]
                    for j, b in enumerate(here):
                        v.tensor_copy(place(tile_hi, h, j), batch_at(b)).then_inc(tile_hi_ready, 1)
                    dve.wait_ge(tile_hi_ready, TB * t + TB)
                    for j, b in enumerate(here):
                        hi = place(tile_hi, h, j)
                        v.tensor_tensor(place(tile_lo, h, j), batch_at(b), hi.bitcast(F32),
                                        ALU.subtract).then_inc(tile_ready, 1)

            dve.wait_ge(tables_ready, 1)
            pairs_n = dve.value_load(pairs_i[0:1, 0:1], min_val=B // TB // 2, max_val=MAX_TILES // 2)
            quads_n = pairs_n // 2
            dve.wait_ge(x1_ready, CHUNKS * K)
            some_tiles(0, TILE_BUFS, first_batches)
            with dve.Fori(1, quads_n) as i:
                some_tiles(i, TILE_BUFS, x1_batches(i * TILE_BUFS, TILE_BUFS))
            with dve.If(pairs_n > quads_n * 2):
                some_tiles(quads_n, 2, x1_batches(quads_n * TILE_BUFS, 2))

        @block.tensor
        def _(pe):
            mm = nc.tensor.matmul
            pe.nop().then_inc(tiles_done, TILE_BUFS)

            def lora(m):
                if m >= 2:
                    pe.wait_ge(delta_ready, m - 1)
                mm(ps_d[:, m % 2, :], lb[:, m * P:(m + 1) * P], la, start=True, stop=True).then_inc(delta_ps, 1)

            def turn(m):
                pe.wait_ge(weff_ready, m + 1)
                if m >= 1:
                    pe.wait_ge(w0_ready, m)
                for k in range(K):
                    to = ps_w[:, k * P:(k + 1) * P]
                    last = mm(to, quant[:, m, k * P:(k + 1) * P], ident[:, :], start=True, stop=(k != m))
                    if k == m:
                        last = mm(to, ident[:, :], ident[:, :], start=False, stop=True)
                last.then_inc(turned_ready, 1)

            def layer0(m, c):
                if m == 0:
                    pe.wait_ge(x_ready, c + 1)
                else:
                    pe.wait_ge(x1_ready, c + (CHUNKS * (m - 1) + 1))
                for n, (w, low) in enumerate(((w0_hi, 0), (w0_lo, 0), (w0_hi, ROW))):
                    for k in range(K):
                        cols = pairs[:, bass.ds(c * (2 * ROW) + (FIRST * 2 * ROW + low), ROW)]
                        cols = cols.rearrange("p (q k s) -> p q k s", k=K, s=S)[:, :, k, :]
                        last = mm(ps0[:, bass.ds(c, 1), :].rearrange("p c n -> p (c n)"),
                                  w[:, m % 2, k * P:(k + 1) * P], cols,
                                  start=(n == 0 and k == 0), stop=(n == 2 and k == K - 1))
                last.then_inc(l0_done, 1)

            pe.wait_ge(lora_in, 32)
            lora(0)
            pe.wait_ge(members_ready, 1)
            mm(counts_ps[:, 0, :], ones[:, :], is_adapter[:, :], start=True, stop=True)
            mm(counts_ps[:, 1, :], earlier[:, :], is_adapter[:, :], start=True, stop=True).then_inc(counts_ps_ready, 1)
            for m in range(1, K):
                lora(m)
            pe.wait_ge(ident_ready, 1)
            turn(0)
            for m in range(K):
                pe.wait_ge(w0_ready, m + 1)
                with pe.Fori(0, CHUNKS - 1) as c:
                    layer0(m, c)
                if m + 1 < K:
                    turn(m + 1)
                layer0(m, CHUNKS - 1)
                if m == K - 2:
                    pe.wait_ge(slots_ready, 1)
                    pe.wait_ge(delta_ready, K)
                    mm(batch_ps, i_col_b[0:B, :], at_slot[:, :], start=True, stop=True).then_inc(slots_ps, 1)

            pe.wait_ge(tables_ready, 1)
            pairs_n = pe.value_load(pairs_i[0:1, 0:1], min_val=B // TB // 2, max_val=MAX_TILES // 2)

            def some_tiles(i, n):
                of_tiles = load_values(pe, tile_i[0:1, bass.ds(TILE_BUFS * i, n)], 0, RING * NA - 1)
                for h in range(n):
                    t = TILE_BUFS * i + h
                    pe.wait_ge(tile_ready, TB * t + TB)
                    pe.wait_ge(split_pool, of_tiles[h] // RING + 1)
                    pe.wait_ge(y_ready, t + 1)
                    at = of_tiles[h] % RING * (2 * ROW)
                    parts = ((tile_hi, 0), (tile_lo, 0), (tile_hi, ROW))
                    for n, (xs, low) in enumerate(parts):
                        for k in range(K):
                            last = mm(ps_y[:, h, :], xs[:, h, k * P:(k + 1) * P],
                                      pairs[:, bass.ds(at + (low + k * D), D)],
                                      start=(n == 0 and k == 0), stop=(n == 2 and k == K - 1))
                    last.then_inc(tiles_done, 1)

            assert TILE_BUFS == YB == 4
            quads_n = pairs_n // 2
            with pe.Fori(0, quads_n) as i:
                some_tiles(i, TILE_BUFS)
            with pe.If(pairs_n > quads_n * 2):
                some_tiles(quads_n, 2)


def kernel(x, condB_codebook, itok_B_0_15, L0_cond_weight, L0_cond_scale_log, L0_cond_lora_A, L0_cond_lora_B,
           L1_cond_weight):
    import numpy as np
    import concourse.bacc as bacc
    from concourse.bass_utils import run_bass_kernel_spmd as run

    arrays = {
        "x_t": x.reshape(B, S, K, P).transpose(0, 3, 2, 1).reshape(B, P, BLK),
        "codebook": condB_codebook,
        "ids": itok_B_0_15,
        "w0": L0_cond_weight,
        "scales": L0_cond_scale_log.reshape(K, P, K).transpose(1, 0, 2),
        "lora_a": L0_cond_lora_A,
        "lora_bt": L0_cond_lora_B.T,
        "w1_t": L1_cond_weight.reshape(NA, D, K, P).transpose(0, 3, 2, 1).reshape(NA, P, ROW),
    }
    arrays = {name: np.ascontiguousarray(a) for name, a in arrays.items()}
    nc = bacc.Bacc("TRN2", target_bir_lowering=False, num_devices=1)
    args = [nc.dram_tensor(name, a.shape, mybir.dt.from_np(a.dtype), kind="ExternalInput").ap()
            for name, a in arrays.items()]
    out = nc.dram_tensor("result", (B, S, D), F32, kind="ExternalOutput").ap()
    adapter_mlp(nc, *args, out)
    return run(nc, [arrays], core_ids=[0]).results[0]["result"]
```
